# Optimizing a Trainium2 kernel written in Bass

```python
import numpy as np
import jax
import jax.numpy as jnp

def _softmax(x, axis=-1):
    return jax.nn.softmax(x, axis=axis)

def _gelu(x):
    return jax.nn.gelu(x, approximate=True)

def _silu(x):
    return jax.nn.silu(x)

def _sigmoid(x):
    return jax.nn.sigmoid(x)

def _layernorm(x, axis=-1, eps=1e-05):
    m = jnp.mean(x, axis=axis, keepdims=True)
    v = jnp.var(x, axis=axis, keepdims=True)
    return (x - m) / jnp.sqrt(v + eps)

def _scatter_add(tgt, idx, src, axis=0):
    return tgt.at[idx].add(src)

def _segment_sum(src, seg, n):
    return jax.ops.segment_sum(src, seg, n)
kernel_name = 'mk_gnn_resnorm_d4_gnn_r8_b88964'

def setup_inputs(seed: int=0):
    np.random.seed(seed)
    _w = jnp.asarray

    def _rec_inputs():
        import jax
        import jax.numpy as jnp
        _gk = jax.random.key(seed)
        x = -0.0001006 + 1 * jax.random.normal(jax.random.fold_in(_gk, 1), (12500, 48), jnp.float32)
        _s = jax.random.randint(jax.random.fold_in(_gk, 2), (100000,), 0, 12500, jnp.int32)
        _d = jax.random.randint(jax.random.fold_in(_gk, 3), (100000,), 0, 12500, jnp.int32)
        _loop = jnp.arange(12500, dtype=jnp.int32)
        src = jnp.concatenate([_s, _d, _loop])
        dst = jnp.concatenate([_d, _s, _loop])
        _o = jnp.argsort(dst, stable=True)
        src = src[_o]
        dst = dst[_o]
        edge_attr_48 = -4.21973e-05 + 0.999841 * jax.random.normal(jax.random.fold_in(_gk, 12), (212500, 48), jnp.float32)
        edge_weight = jax.random.uniform(jax.random.fold_in(_gk, 14), (212500,), jnp.float32, 0.0, 0.999998)
        return (x, src, dst, edge_attr_48, edge_weight)
    x, src, dst, edge_attr_48, edge_weight = _rec_inputs()

    def _L0_gnn_setup():
        import jax, jax.numpy as jnp
        import numpy as np
        N_NODES = 12500
        N_EDGES = 200000
        D_FEAT = 48
        key = jax.random.key(seed)
        k1, k2, k3, k4 = jax.random.split(key, 4)
        node_feat = jax.random.normal(k1, (N_NODES, D_FEAT), dtype=jnp.float32)
        edge_feat = jax.random.normal(k2, (N_EDGES, D_FEAT), dtype=jnp.float32)
        src = jax.random.randint(k3, (N_EDGES,), 0, N_NODES, dtype=jnp.int32)
        dst = jax.random.randint(k4, (N_EDGES,), 0, N_NODES, dtype=jnp.int32)
        eps = jnp.zeros((1,), dtype=jnp.float32)
        return {'node_feat': node_feat, 'edge_feat': edge_feat, 'src': src, 'dst': dst, 'eps': eps}
    _L0_gnn_all = _L0_gnn_setup()
    _L0_gnn_in = {k: v for k, v in _L0_gnn_all.items() if k in ('eps',)}
    del _L0_gnn_all

    def _L1_gnn_setup():
        import jax, jax.numpy as jnp
        import numpy as np
        N_NODES = 12500
        N_EDGES = 200000
        D_FEAT = 48
        N_LAYERS = 2
        key = jax.random.key(seed)
        k1, k2, k3 = jax.random.split(key, 3)
        row = jax.random.randint(k1, (N_EDGES,), 0, N_NODES, dtype=jnp.int32)
        col = jax.random.randint(k2, (N_EDGES,), 0, N_NODES, dtype=jnp.int32)
        x = jax.random.normal(k3, (N_NODES, D_FEAT), dtype=jnp.float32)
        return {'row': row, 'col': col, 'x': x}
    _L1_gnn_all = _L1_gnn_setup()
    _L1_gnn_in = {k: v for k, v in _L1_gnn_all.items() if k in ()}
    del _L1_gnn_all

    def _L2_gnn_setup():
        import jax, jax.numpy as jnp
        import numpy as np
        N_NODES = 12500
        N_EDGES = 200000
        D_IN = 48
        D_H = 48
        D_OUT = 48

        def _graph_conv(x, src, dst, w_rel, w_root, b, num_nodes):
            agg = jax.ops.segment_sum(x[src], dst, num_segments=num_nodes)
            return agg @ w_rel + x @ w_root + b
        key = jax.random.key(seed)
        ks = jax.random.split(key, 8)
        s = 0.05
        x = jax.random.normal(ks[0], (N_NODES, D_IN), dtype=jnp.float32)
        edge_index = jax.random.randint(ks[1], (2, N_EDGES), 0, N_NODES, dtype=jnp.int64)
        w_rel1 = jax.random.normal(ks[2], (D_IN, D_H), dtype=jnp.float32) * s
        w_root1 = jax.random.normal(ks[3], (D_IN, D_H), dtype=jnp.float32) * s
        b1 = jax.random.normal(ks[4], (D_H,), dtype=jnp.float32) * s
        w_rel2 = jax.random.normal(ks[5], (D_H, D_OUT), dtype=jnp.float32) * s
        w_root2 = jax.random.normal(ks[6], (D_H, D_OUT), dtype=jnp.float32) * s
        b2 = jax.random.normal(ks[7], (D_OUT,), dtype=jnp.float32) * s
        return {'x': x, 'edge_index': edge_index, 'w_rel1': w_rel1, 'w_root1': w_root1, 'b1': b1, 'w_rel2': w_rel2, 'w_root2': w_root2, 'b2': b2}
    _L2_gnn_all = _L2_gnn_setup()
    _L2_gnn_in = {k: v for k, v in _L2_gnn_all.items() if k in ('w_rel1', 'w_root1', 'b1', 'w_rel2', 'w_root2', 'b2')}
    del _L2_gnn_all

    def _L3_gnn_setup():
        import jax, jax.numpy as jnp
        import numpy as np
        N_NODES = 12500
        N_EDGES = 200000
        D_IN = 48
        D_OUT = 48
        key = jax.random.key(seed)
        k1, k2, k3, k4, k5 = jax.random.split(key, 5)
        x = jax.random.normal(k1, (N_NODES, D_IN), dtype=jnp.float32)
        init_range = np.sqrt(6.0 / (D_IN + D_OUT)).astype(np.float32)
        w = jax.random.uniform(k2, (D_IN, D_OUT), dtype=jnp.float32, minval=-init_range, maxval=init_range)
        b = jnp.zeros((D_OUT,), dtype=jnp.float32)
        edge_src = jax.random.randint(k3, (N_EDGES,), 0, N_NODES, dtype=jnp.int32)
        edge_dst = jax.random.randint(k4, (N_EDGES,), 0, N_NODES, dtype=jnp.int32)
        adj_vals = jax.random.uniform(k5, (N_EDGES,), dtype=jnp.float32)
        return {'x': x, 'w': w, 'b': b, 'edge_src': edge_src, 'edge_dst': edge_dst, 'adj_vals': adj_vals}
    _L3_gnn_all = _L3_gnn_setup()
    _L3_gnn_in = {k: v for k, v in _L3_gnn_all.items() if k in ('w', 'b')}
    del _L3_gnn_all
    return {'x': x, 'src': src, 'dst': dst, 'edge_attr_48': edge_attr_48, 'edge_weight': edge_weight, 'L0_gnn_eps': _L0_gnn_in['eps'], 'L2_gnn_w_rel1': _L2_gnn_in['w_rel1'], 'L2_gnn_w_root1': _L2_gnn_in['w_root1'], 'L2_gnn_b1': _L2_gnn_in['b1'], 'L2_gnn_w_rel2': _L2_gnn_in['w_rel2'], 'L2_gnn_w_root2': _L2_gnn_in['w_root2'], 'L2_gnn_b2': _L2_gnn_in['b2'], 'L3_gnn_w': _L3_gnn_in['w'], 'L3_gnn_b': _L3_gnn_in['b']}

def reference(x, src, dst, edge_attr_48, edge_weight, L0_gnn_eps, L2_gnn_w_rel1, L2_gnn_w_root1, L2_gnn_b1, L2_gnn_w_rel2, L2_gnn_w_root2, L2_gnn_b2, L3_gnn_w, L3_gnn_b):
    import jax
    import jax.numpy as jnp

    def _L0_gnn_ref(node_feat, edge_feat, src, dst, eps):
        import jax, jax.numpy as jnp
        import numpy as np
        N_NODES = 12500
        N_EDGES = 200000
        D_FEAT = 48
        m = jax.nn.relu(node_feat[src] + edge_feat)
        neigh = jax.ops.segment_sum(m, dst, num_segments=N_NODES)
        return (1.0 + eps[0]) * node_feat + neigh

    def _L1_gnn_ref(row, col, x):
        import jax, jax.numpy as jnp
        import numpy as np
        N_NODES = 12500
        N_EDGES = 200000
        D_FEAT = 48
        N_LAYERS = 2
        n = x.shape[0]
        loop = jnp.arange(n, dtype=row.dtype)
        r = jnp.concatenate([row, loop])
        c = jnp.concatenate([col, loop])
        deg = jax.ops.segment_sum(jnp.ones(r.shape, dtype=x.dtype), r, num_segments=n)
        dinv = jnp.where(deg > 0, jax.lax.rsqrt(deg), 0.0)
        w = dinv[r] * dinv[c]
        for _ in range(N_LAYERS):
            x = jax.ops.segment_sum(w[:, None] * x[c], r, num_segments=n)
        return x

    def _L2_gnn_ref(x, edge_index, w_rel1, w_root1, b1, w_rel2, w_root2, b2):
        import jax, jax.numpy as jnp
        import numpy as np
        N_NODES = 12500
        N_EDGES = 200000
        D_IN = 48
        D_H = 48
        D_OUT = 48

        def _graph_conv(x, src, dst, w_rel, w_root, b, num_nodes):
            agg = jax.ops.segment_sum(x[src], dst, num_segments=num_nodes)
            return agg @ w_rel + x @ w_root + b
        src, dst = (edge_index[0], edge_index[1])
        n = x.shape[0]
        h = jax.nn.relu(_graph_conv(x, src, dst, w_rel1, w_root1, b1, n))
        out = _graph_conv(h, src, dst, w_rel2, w_root2, b2, n)
        return out

    def _L3_gnn_ref(x, w, b, edge_src, edge_dst, adj_vals):
        import jax, jax.numpy as jnp
        import numpy as np
        N_NODES = 12500
        N_EDGES = 200000
        D_IN = 48
        D_OUT = 48
        xw = jnp.matmul(x, w)
        msgs = adj_vals[:, None] * xw[edge_src]
        agg = jax.ops.segment_sum(msgs, edge_dst, num_segments=N_NODES)
        return jax.nn.relu(agg + b)
    edge_index = jnp.stack([src, dst])
    x = _layernorm(x + _L0_gnn_ref(x, edge_attr_48, src, dst, L0_gnn_eps), axis=-1)
    x = _layernorm(x + _L1_gnn_ref(src, dst, x), axis=-1)
    x = _layernorm(x + _L2_gnn_ref(x, edge_index, L2_gnn_w_rel1, L2_gnn_w_root1, L2_gnn_b1, L2_gnn_w_rel2, L2_gnn_w_root2, L2_gnn_b2), axis=-1)
    x = _layernorm(x + _L3_gnn_ref(x, L3_gnn_w, L3_gnn_b, src, dst, edge_weight), axis=-1)
    return x

_drawn_inputs = setup_inputs


def setup_inputs(seed=0):
    import zlib

    import numpy as np

    out = dict(_drawn_inputs(seed))
    spreads = {'L3_gnn_b': (0.0, 0.731)}
    factors = {'L2_gnn_b2': 3.458}
    for name, (base, spread) in spreads.items():
        noise = np.random.default_rng([zlib.crc32(name.encode()), seed]).standard_normal(out[name].shape)
        drawn = base * np.exp(spread * noise) if base else spread * noise
        out[name] = jnp.asarray(drawn.astype(out[name].dtype))
    for name, factor in factors.items():
        out[name] = (out[name] * factor).astype(out[name].dtype)
    return out
```

```python
import concourse.bass as bass
from concourse import mybir
from contextlib import ExitStack

F32 = mybir.dt.float32
BF16 = mybir.dt.bfloat16
I32 = mybir.dt.int32
U16 = mybir.dt.uint16
ALU = mybir.AluOpType
ACT = mybir.ActivationFunctionType
AX = mybir.AxisListType

N, E, D = 12500, 212500, 48
P = 125
NB = N // P
EC = E // P
T = 128
GT = 16
NG = 2 * -(-((E + (T - 1) * NB) // T) // (2 * GT))
NT = NG * GT
SLOTS = NT * T
ROW = D + 3
SC = 17
CT = 440
QB = 4
EPS = 1e-5
DST, SRC = 0, 1
PASSES = [(DST, "edge"), (SRC, "plain"), (SRC, "plain"), (DST, "plain"), (DST, "plain"), (DST, "weight")]


def rounds(engine, n, body):
    body(0)
    with engine.Fori(1, n) as i:
        body(i)


def wait_past(engine, semaphore, count):
    if not isinstance(count, int) or count > 0:
        engine.wait_ge(semaphore, count)


def gnn_program(nc, x_in, src_in, dst_in, ea_in, w_in, eps_in, w_rel1, w_root1, b1, w_rel2, w_root2, b2,
                w3, b3, out):
    assert NB * P == N and EC * P == E and EC % (2 * SC) == 0 and SLOTS >= E + (T - 1) * NB
    assert NT % CT == 0 and NB % QB == 0
    ds = bass.ds
    with ExitStack() as ctx:
        def sb(name, shape, dt=F32):
            return ctx.enter_context(nc.sbuf_tensor(name, shape, dt))

        def ps(name, shape):
            return ctx.enter_context(nc.psum_tensor(name, shape, F32))

        def sem(name):
            return ctx.enter_context(nc.semaphore(name))

        rows_dram = nc.dram_tensor("edge_rows", (SLOTS, ROW), F32).ap()
        back_dram = nc.dram_tensor("back_rows", (SLOTS, 2), I32).ap()
        table = [nc.dram_tensor(f"node_table{k}", (N, D), F32).ap() for k in range(len(PASSES))]

        ones = sb("ones", [128, 128])
        before = sb("before", [128, 128])
        ident = sb("ident", [128, 128])
        lane = sb("lane", [128, P])
        X = sb("X", [P, NB * D])
        AGG = sb("AGG", [P, NB * D])
        TMP = sb("TMP", [128, NB * D])
        EDGE = sb("EDGE", [P, 3 * EC])
        H = EDGE[:, 0:NB * D]
        stat = sb("stat", [P, 4, NB])
        dinv = sb("dinv", [P, NB])
        eps_sb = sb("eps_sb", [P, 1])
        bias = sb("bias", [P, 3, D])
        weights = sb("weights", [D, 5, D])
        src_i = EDGE[:, 0:EC].bitcast(I32)
        dst_i = EDGE[:, EC:2 * EC].bitcast(I32)
        w_e = EDGE[:, 2 * EC:3 * EC]
        node_of = [dst_i, src_i]
        part = [sb(f"part{k}", [P, EC]) for k in range(2)]
        blk = [sb(f"blk{k}", [P, EC], BF16) for k in range(2)]
        row_at = [sb(f"row_at{k}", [P, EC], I32) for k in range(2)]
        mask = [sb(f"mask{k}", [P, EC], BF16) for k in range(2)]
        scan = [AGG[:, k * EC:(k + 1) * EC] for k in range(2)]
        pos = TMP[0:P, 0:EC]
        hist = sb("hist", [P, NB])
        off = sb("off", [P, NB])
        cnt_i = sb("cnt_i", [NB, 1], I32)
        cnt_f = sb("cnt_f", [NB, 1])
        start_f = sb("start_f", [NB, 1])
        dstart = sb("dstart", [NB, NB])
        tile_no = sb("tile_no", [NB, CT])
        begun = sb("begun", [NB, CT])
        row_store = [sb(f"row_store{k}", [128, SC, ROW]) for k in range(2)]
        rowbuf = [r[0:P, :, :] for r in row_store]
        backbuf = [sb(f"backbuf{k}", [P, SC, 2], I32) for k in range(2)]
        at_stage = [sb(f"at_stage{k}", [P, SC], I32) for k in range(2)]
        TMPB = TMP[:, :].bitcast(BF16)
        deg_p = [TMPB[0:P, k * SC * P:(k + 1) * SC * P].rearrange("p (c m) -> p c m", m=P) for k in range(2)]
        deg_b = [TMPB[0:P, 2 * SC * P + k * SC * NB:2 * SC * P + (k + 1) * SC * NB]
                 .rearrange("p (c m) -> p c m", m=NB) for k in range(2)]
        raw_back = sb("raw_back", [128, NG, GT, 2], I32)
        idx_dst = sb("idx_dst", [128, NT], I32)
        lo = [sb(f"lo{k}", [128, NT]) for k in range(2)]
        w_s = sb("w_s", [128, NT])
        tile_block = [sb(f"tile_block{k}", [1, NT], I32) for k in range(2)]
        fill = sb("fill", [128, GT, ROW])
        fill_back = sb("fill_back", [128, GT, 2], I32)
        rows = [r[:, 0:GT, :] for r in row_store]
        msg = [sb(f"msg{k}", [128, GT, D]) for k in range(2)]
        onehot = [TMP[:, k * GT * P:(k + 1) * GT * P].rearrange("p (j m) -> p j m", m=P) for k in range(2)]
        idx_stage = [sb(f"idx_stage{k}", [128, GT], I32) for k in range(2)]
        quad = [sb(f"quad{k}", [P, QB * D]) for k in range(2)]
        tT = [sb(f"tT{k}", [D, QB * P]) for k in range(2)]

        pacc = [ps(f"pacc{k}", [128, 2, 512]) for k in range(2)]
        ptr = [ps(f"ptr{k}", [128, 512]) for k in range(2)]
        pout = ps("pout", [128, 512])
        psort = ps("psort", [128, 512])

        s_edges = sem("edges_loaded")
        s_x = sem("x_loaded")
        s_small = sem("small_loaded")
        s_const = sem("constants_ready")
        s_fill = sem("fill_ready")
        s_filled = sem("dram_filled")
        s_dve = sem("vector_step")
        s_pool_turn, s_dve_turn, s_pe_turn = sem("gpsimd_turn"), sem("vector_turn"), sem("tensor_turn")
        s_hist = sem("histogram_ready")
        s_cnt = sem("counts_summed")
        s_tiles = sem("tile_counts_ready")
        s_start = sem("starts_summed")
        s_dstart = sem("starts_ready")
        s_off = sem("offsets_summed")
        s_begun = sem("begun_ready")
        s_blocks = sem("blocks_counted")
        s_row_at = sem("row_positions_ready")
        s_staged = [[sem(f"scatter_staged{d}_{k}") for k in range(2)] for d in range(2)]
        s_eaload = [sem(f"edge_features_loaded{k}") for k in range(2)]
        s_scat = [[sem(f"scattered{d}_{k}") for k in range(2)] for d in range(2)]
        s_degoh = [sem(f"degree_onehots_ready{k}") for k in range(2)]
        s_degmm = [sem(f"degree_onehots_used{k}") for k in range(2)]
        s_deg = sem("degrees_summed")
        s_back = sem("back_rows_loaded")
        s_table_ready = sem("table_values_ready")
        s_table = sem("table_written")
        s_rows = [sem(f"rows_loaded{k}") for k in range(2)]
        s_idx = [[sem(f"indices_staged{q}_{k}") for k in range(2)] for q in range(len(PASSES))]
        s_gath = [[sem(f"gathered{q}_{k}") for k in range(2)] for q in range(len(PASSES))]
        s_msg = [[sem(f"messages_ready{q}_{k}") for k in range(2)] for q in range(len(PASSES))]
        s_oh = [[sem(f"onehot_ready{q}_{k}") for k in range(2)] for q in range(len(PASSES))]
        s_sum = [[sem(f"tiles_summed{q}_{k}") for k in range(2)] for q in range(len(PASSES))]
        s_added = [[sem(f"sums_added{q}_{k}") for k in range(2)] for q in range(len(PASSES))]
        s_var = sem("variance_ready")
        s_std = sem("deviation_ready")
        s_node = sem("node_values_ready")
        s_quad = sem("blocks_staged")
        s_tr = sem("blocks_transposed")
        s_trc = sem("transposes_copied")
        s_mm = sem("blocks_multiplied")
        s_mmu = sem("products_used")
        s_res = sem("result_ready")
        s_out = sem("output_written")

        HALF = EC // (2 * SC)
        PAIRS = NG // 2
        QUADS = NB // QB
        rows_g = rows_dram.rearrange("(g p j) c -> g p (j c)", p=128, j=GT)
        back_g = back_dram.rearrange("(g p j) c -> p g (j c)", p=128, j=GT)
        ea_c = ea_in.rearrange("(p c) f -> p c f", p=P)
        TRANSFORMS = [(0, 1), (2, 3), (4, None)]

        block = ctx.enter_context(nc.Block())

        @block.sync
        def _(sp):
            sp.dma_start(dst_i, dst_in.rearrange("(p c) -> p c", p=P)).then_inc(s_edges, 16)
            sp.dma_start(src_i, src_in.rearrange("(p c) -> p c", p=P)).then_inc(s_edges, 16)
            sp.dma_start(w_e, w_in.rearrange("(p c) -> p c", p=P)).then_inc(s_edges, 16)
            sp.wait_ge(s_fill, 1)
            sp.dma_start(rows_dram.rearrange("(g p j) c -> p g (j c)", p=128, j=GT),
                         fill[:, :, :].rearrange("p j c -> p (j c)").unsqueeze(1)
                         .to_broadcast([128, NG, GT * ROW])).then_inc(s_filled, 16)
            sp.dma_start(back_g, fill_back[:, :, :].rearrange("p j c -> p (j c)").unsqueeze(1)
                         .to_broadcast([128, NG, GT * 2])).then_inc(s_filled, 16)
            sp.dma_start(X[:, :], x_in.rearrange("(p b) f -> p (b f)", p=P)).then_inc(s_x, 16)
            for k, w in enumerate((w_rel1, w_root1, w_rel2, w_root2, w3)):
                sp.dma_start(weights[:, k, :], w).then_inc(s_small, 16)
            for k, b in enumerate((b1, b2, b3)):
                sp.dma_start(bias[:, k, :], b.rearrange("(a n) -> a n", a=1).to_broadcast([P, D])).then_inc(s_small, 16)
            sp.dma_start(eps_sb[:, :], eps_in.rearrange("(a n) -> a n", a=1).to_broadcast([P, 1])).then_inc(s_small, 16)
            def one_round(i):
                for s in range(2):
                    wait_past(sp, s_scat[DST][s], i * (16 * SC))
                    sp.dma_start(rowbuf[s][:, :, 0:D], ea_c[:, ds(i * (2 * SC) + s * SC, SC), :]).then_inc(s_eaload[s], 16)

            rounds(sp, HALF, one_round)
            for s in range(2):
                sp.wait_ge(s_scat[SRC][s], HALF * 16 * SC)
            sp.dma_start(raw_back[:, :, :, :].rearrange("p g j c -> p g (j c)"), back_g).then_inc(s_back, 16)
            for q, (_, kind) in enumerate(PASSES):
                sp.wait_ge(s_table_ready, q + 1)
                if q == 0:
                    sp.wait_ge(s_x, 16)
                sp.dma_start(table[q].rearrange("(p b) f -> p (b f)", p=P),
                             H if kind == "plain" and q != 3 else X[:, :]).then_inc(s_table, 16)
                if kind == "edge":
                    for s in range(2):
                        sp.wait_ge(s_scat[DST][s], HALF * 16 * SC)
                    def one_round(i):
                        for s in range(2):
                            wait_past(sp, s_msg[q][s], i)
                            sp.dma_start(rows[s][:, :, :].rearrange("p j c -> p (j c)"),
                                         rows_g[ds(i * 2 + s, 1), :, :].rearrange("a p c -> (a p) c")).then_inc(s_rows[s], 16)

                    rounds(sp, PAIRS, one_round)
            sp.wait_ge(s_res, 1)
            sp.dma_start(out.rearrange("(p b) f -> p (b f)", p=P), X[:, :]).then_inc(s_out, 16)
            sp.wait_ge(s_filled, 32)
            sp.wait_ge(s_table, 16 * len(PASSES))
            sp.wait_ge(s_out, 16)

        @block.gpsimd
        def _(pool):
            pool.memset(ones[:, :], 1.0).then_inc(s_const, 1)
            pool.iota(lane[:, :], [[1, P]], base=0, channel_multiplier=0,
                      allow_small_or_imprecise_dtypes=True).then_inc(s_const, 1)
            pool.iota(tile_no[:, :], [[1, CT]], base=0, channel_multiplier=0,
                      allow_small_or_imprecise_dtypes=True).then_inc(s_const, 1)
            pool.memset(before[:, :], 1.0).then_inc(s_const, 1)
            pool.memset(ident[:, :], 1.0).then_inc(s_const, 1)
            pool.wait_ge(s_const, 5)
            pool.affine_select(out=before[:, :], in_=before[:, :], compare_op=ALU.is_gt, fill=0.0, base=0,
                               pattern=[[1, 128]], channel_multiplier=-1).then_inc(s_const, 1)
            pool.affine_select(out=ident[:, :], in_=ident[:, :], compare_op=ALU.is_equal, fill=0.0, base=0,
                               pattern=[[1, 128]], channel_multiplier=-1).then_inc(s_const, 1)
            for d in (DST, SRC):
                bufs, target = ((rowbuf, rows_dram), (backbuf, back_dram))[d]
                def one_round(i):
                    for s in range(2):
                        pool.wait_ge(s_staged[d][s], i + 1)
                        if d == DST:
                            pool.wait_ge(s_eaload[s], i * 16 + 16)
                        pool.wait_ge(s_filled, 32)
                        pool.sem_inc(s_pool_turn, 1)
                        for j in range(SC):
                            pool.indirect_dma_start(
                                target, bass.IndirectOffsetOnAxis(ap=at_stage[s][:, j:j + 1], axis=0),
                                bufs[s][:, j, :], None).then_inc(s_scat[d][s], 16)

                rounds(pool, HALF, one_round)
            for q in range(len(PASSES)):
                def one_round(i):
                    for s in range(2):
                        pool.wait_ge(s_idx[q][s], i + 1)
                        wait_past(pool, s_sum[q][s], i)
                        pool.wait_ge(s_table, 16 * (q + 1))
                        pool.sem_inc(s_pool_turn, 1)
                        for j in range(GT):
                            pool.indirect_dma_start(
                                msg[s][:, j, :], None, table[q],
                                bass.IndirectOffsetOnAxis(ap=idx_stage[s][:, j:j + 1], axis=0)).then_inc(s_gath[q][s], 16)

                rounds(pool, PAIRS, one_round)

        @block.scalar
        def _(act):
            for d in (DST, SRC):
                act.wait_ge(s_row_at, d + 1)
                if d == SRC:
                    for s in range(2):
                        act.wait_ge(s_scat[DST][s], HALF * 16 * SC)
                def one_round(i):
                    for s in range(2):
                        wait_past(act, s_scat[d][s], i * (16 * SC))
                        cols = ds(i * (2 * SC) + s * SC, SC)
                        act.copy(at_stage[s][:, :], row_at[d][:, cols])
                        if d == DST:
                            act.copy(rowbuf[s][:, :, D:D + 1].bitcast(I32), src_i[:, cols].unsqueeze(2))
                            act.copy(rowbuf[s][:, :, D + 1:D + 2], part[DST][:, cols].unsqueeze(2))
                            act.copy(rowbuf[s][:, :, D + 2:D + 3], w_e[:, cols].unsqueeze(2)).then_inc(s_staged[d][s], 1)
                        else:
                            act.copy(backbuf[s][:, :, 0:1], dst_i[:, cols].unsqueeze(2))
                            act.copy(backbuf[s][:, :, 1:2], part[SRC][:, cols].unsqueeze(2)).then_inc(s_staged[d][s], 1)

                rounds(act, HALF, one_round)
            sqrts = 0

            def sqrt(out_, in_):
                nonlocal sqrts
                sqrts += 1
                act.wait_ge(s_var, sqrts)
                act.activation(out_, in_, ACT.Sqrt).then_inc(s_std, 1)

            def copy_transposes(t):
                own = TRANSFORMS[t][1] is not None
                act.wait_ge(s_node, t + 1)
                def one_round(i):
                    wait_past(act, s_tr, i + t * QUADS)
                    cols = ds(i * (QB * D), QB * D)
                    if own:
                        act.copy(quad[1][:, :], (X[:, :], H)[t][:, cols])
                    act.copy(quad[0][:, :], AGG[:, cols]).then_inc(s_quad, 1)
                    act.wait_ge(s_tr, i + (t * QUADS + 1))
                    wait_past(act, s_mm, i + t * QUADS)
                    if own:
                        act.copy(tT[1][:, :], ptr[1][0:D, 0:QB * P])
                    act.copy(tT[0][:, :], ptr[0][0:D, 0:QB * P]).then_inc(s_trc, 1)

                rounds(act, QUADS, one_round)

            for q, (d, kind) in enumerate(PASSES):
                if q == 1:
                    act.wait_ge(s_back, 16)
                if q > 0:
                    for s in range(2):
                        act.wait_ge(s_gath[q - 1][s], PAIRS * 16 * GT)
                def one_round(i):
                    for s in range(2):
                        cols = ds(i * (2 * GT) + s * GT, GT)
                        wait_past(act, s_gath[q][s], i * (16 * GT))
                        if kind == "edge":
                            act.wait_ge(s_rows[s], i * 16 + 16)
                            act.copy(idx_stage[s][:, :].unsqueeze(2), rows[s][:, :, D:D + 1].bitcast(I32))
                            act.copy(idx_dst[:, cols].unsqueeze(2), rows[s][:, :, D:D + 1].bitcast(I32))
                            act.copy(lo[DST][:, cols].unsqueeze(2), rows[s][:, :, D + 1:D + 2])
                            act.copy(w_s[:, cols].unsqueeze(2), rows[s][:, :, D + 2:D + 3]).then_inc(s_idx[q][s], 1)
                        elif d == DST:
                            act.copy(idx_stage[s][:, :], idx_dst[:, cols]).then_inc(s_idx[q][s], 1)
                        else:
                            act.copy(idx_stage[s][:, :].unsqueeze(2),
                                     raw_back[:, :, :, :].rearrange("p g j c -> p (g j) c")[:, cols, 0:1]).then_inc(s_idx[q][s], 1)

                rounds(act, PAIRS, one_round)
                if q == 0:
                    sqrt(stat[:, 2, :], stat[:, 1, :])
                    sqrt(dinv[:, :], dinv[:, :])
                if q == 2:
                    sqrt(stat[:, 2, :], stat[:, 1, :])
                if q >= 3:
                    copy_transposes(q - 3)
                if q >= 4:
                    sqrt(stat[:, 2, :], stat[:, 1, :])

        @block.tensor
        def _(pe):
            pe.wait_ge(s_const, 7)
            for d in (DST, SRC):
                pe.wait_ge(s_hist, d + 1)
                pe.matmul(psort[0:NB, 0:1], hist[:, :], ones[0:P, 0:1], start=True, stop=True).then_inc(s_cnt, 1)
                pe.wait_ge(s_tiles, d + 1)
                pe.matmul(psort[0:NB, 1:2], before[0:NB, 0:NB], cnt_f[:, :], start=True, stop=True).then_inc(s_start, 1)
                pe.wait_ge(s_dstart, d + 1)
                pe.matmul(psort[0:P, 128:128 + NB], before[0:P, 0:P], hist[:, :], start=True, stop=False)
                pe.matmul(psort[0:P, 128:128 + NB], ones[0:NB, 0:P], dstart[:, :], start=False, stop=True).then_inc(s_off, 1)
                for c in range(NT // CT):
                    n = d * (NT // CT) + c + 1
                    pe.wait_ge(s_begun, n)
                    pe.matmul(ptr[0][0:1, 0:CT], ones[0:NB, 0:1], begun[:, :], start=True, stop=True).then_inc(s_blocks, 1)
            pe.wait_ge(s_degoh[0], 1)
            for s in range(2):
                pe.wait_ge(s_degoh[s], 1)
                for c in range(SC):
                    m = pe.matmul(pout[0:P, 0:NB], deg_p[s][:, c, :], deg_b[s][:, c, :], start=(s == 0 and c == 0), stop=False)
                m.then_inc(s_degmm[s], 1)
            with pe.Fori(1, HALF) as i:
                for s in range(2):
                    pe.wait_ge(s_degoh[s], i + 1)
                    for c in range(SC):
                        m = pe.matmul(pout[0:P, 0:NB], deg_p[s][:, c, :], deg_b[s][:, c, :], start=False, stop=False)
                    m.then_inc(s_degmm[s], 1)
            pe.matmul(pout[0:P, 0:NB], ones[0:1, 0:P], ones[0:1, 0:NB], start=False, stop=True).then_inc(s_deg, 1)

            def transform(t):
                rel, root = TRANSFORMS[t]
                pe.wait_ge(s_small, 16 * 9)
                def one_round(i):
                    pe.wait_ge(s_quad, i + (t * QUADS + 1))
                    wait_past(pe, s_trc, i + t * QUADS)
                    pe.sem_inc(s_pe_turn, 1)
                    for b in range(QB):
                        if root is not None:
                            pe.transpose(ptr[1][0:D, b * P:(b + 1) * P], quad[1][:, b * D:(b + 1) * D], ident[0:P, 0:P])
                    for b in range(QB):
                        m = pe.transpose(ptr[0][0:D, b * P:(b + 1) * P], quad[0][:, b * D:(b + 1) * D], ident[0:P, 0:P])
                    m.then_inc(s_tr, 1)
                    pe.wait_ge(s_trc, i + (t * QUADS + 1))
                    wait_past(pe, s_mmu, i + t * QUADS)
                    for b in range(QB):
                        o = pout[0:P, b * D:(b + 1) * D]
                        m = pe.matmul(o, tT[0][:, b * P:(b + 1) * P], weights[:, rel, :], start=True, stop=root is None)
                        if root is not None:
                            m = pe.matmul(o, tT[1][:, b * P:(b + 1) * P], weights[:, root, :], start=False, stop=True)
                    m.then_inc(s_mm, 1)

                rounds(pe, QUADS, one_round)

            for q, (d, kind) in enumerate(PASSES):
                if q > 0:
                    for s in range(2):
                        pe.wait_ge(s_added[q - 1][s], PAIRS)
                def one_round(i):
                    for s in range(2):
                        pe.wait_ge(s_oh[q][s], i + 1)
                        if kind == "plain":
                            pe.wait_ge(s_gath[q][s], i * (16 * GT) + 16 * GT)
                        else:
                            pe.wait_ge(s_msg[q][s], i + 1)
                        wait_past(pe, s_added[q][s], i)
                        for j in range(GT):
                            h, k = divmod(j, GT // 2)
                            m = pe.matmul(pacc[s][0:P, h, k * D:(k + 1) * D], onehot[s][:, j, :], msg[s][:, j, :],
                                          start=True, stop=True)
                        m.then_inc(s_sum[q][s], 1)

                rounds(pe, PAIRS, one_round)
                if q == 3:
                    transform(0)
                if q == 4:
                    transform(1)
                if q == 5:
                    transform(2)

        @block.vector
        def _(dve):
            v = nc.vector
            done = [0]

            def step(ins):
                done[0] += 1
                ins.then_inc(s_dve, 1)
                dve.wait_ge(s_dve, done[0])

            class Loop:
                def __init__(self, i, first, k):
                    self.i, self.base, self.k, self.n = i, done[0] - first * k, k, 0

                def step(self, ins):
                    self.n += 1
                    ins.then_inc(s_dve, 1)
                    dve.wait_ge(s_dve, self.i * self.k + (self.base + self.n))

                def end(self, times):
                    assert self.n == self.k, (self.n, self.k)
                    done[0] += times * self.k

            v.memset(fill[:, :, :], 0.0)
            v.memset(fill_back[:, :, :], 0)
            step(v.memset(mask[0][:, 0:1], 0.0))
            v.memset(fill[:, :, D + 1:D + 2], -1.0)
            v.memset(fill_back[:, :, 1:2], -1).then_inc(s_fill, 1)
            dve.wait_ge(s_edges, 48)
            dve.wait_ge(s_const, 7)
            q_i, r_f = scan[0].bitcast(I32), scan[1]
            for d in (DST, SRC):
                step(v.tensor_scalar(q_i, node_of[d], 1.0 / NB, 0.5 / NB - 0.5, ALU.mult, ALU.add))
                step(v.tensor_copy(part[d][:, :], q_i))
                step(v.scalar_tensor_tensor(r_f, part[d][:, :], -float(NB), node_of[d], ALU.mult, ALU.add))
                step(v.tensor_scalar(pos, r_f, float(NB), None, ALU.is_ge))
                step(v.tensor_tensor(part[d][:, :], part[d][:, :], pos, ALU.add))
                step(v.scalar_tensor_tensor(r_f, pos, -float(NB), r_f, ALU.mult, ALU.add))
                step(v.tensor_scalar(pos, r_f, 0.0, None, ALU.is_lt))
                step(v.tensor_tensor(part[d][:, :], part[d][:, :], pos, ALU.subtract))
                step(v.scalar_tensor_tensor(blk[d][:, :], pos, float(NB), r_f, ALU.mult, ALU.add))
            for d in (DST, SRC):
                with dve.Fori(0, NB // 2) as i:
                    loop = Loop(i, 0, 1)
                    for s in range(2):
                        m = v.tensor_scalar(mask[s][:, :], blk[d][:, :], lane[0:P, ds(i * 2 + s, 1)], 0.0, ALU.is_equal,
                                            ALU.add, accum_out=hist[:, ds(i * 2 + s, 1)])
                    loop.step(m)
                loop.end(NB // 2)
                v.engine_nop().then_inc(s_hist, 1)
                dve.wait_ge(s_cnt, d + 1)
                step(v.tensor_scalar(cnt_i[:, :], psort[0:NB, 0:1], float(T - 1), None, ALU.add))
                step(v.tensor_scalar(cnt_i[:, :], cnt_i[:, :], 7, None, ALU.arith_shift_right))
                v.tensor_copy(cnt_f[:, :], cnt_i[:, :]).then_inc(s_tiles, 1)
                dve.wait_ge(s_start, d + 1)
                step(v.tensor_copy(start_f[:, :], psort[0:NB, 1:2]))
                v.tensor_scalar(dstart[:, :], ident[0:NB, 0:NB], start_f[:, 0:1], float(T), ALU.mult, ALU.mult).then_inc(s_dstart, 1)
                dve.wait_ge(s_off, d + 1)
                step(v.tensor_copy(off[:, :], psort[0:P, 128:128 + NB]))
                for c in range(NT // CT):
                    n = d * (NT // CT) + c + 1
                    v.tensor_scalar(begun[:, :], tile_no[:, :], float(c * CT), start_f[:, 0:1], ALU.add,
                                    ALU.is_ge).then_inc(s_begun, 1)
                    dve.wait_ge(s_blocks, n)
                    step(v.tensor_scalar(tile_block[d][:, c * CT:(c + 1) * CT], ptr[0][0:1, 0:CT], -1.0, None, ALU.add))
                with dve.Fori(0, NB // 2) as i:
                    loop = Loop(i, 0, 4)
                    for s in range(2):
                        m = v.tensor_scalar(mask[s][:, :], blk[d][:, :], lane[0:P, ds(i * 2 + s, 1)], None, ALU.is_equal)
                    loop.step(m)
                    for s in range(2):
                        m = v.tensor_tensor_scan(scan[s], mask[s][:, :], mask[s][:, :], off[:, ds(i * 2 + s, 1)], ALU.add, ALU.max)
                    loop.step(m)
                    for s in range(2):
                        dve.sem_inc(s_dve_turn, 1)
                        loop.step(v.copy_predicated(pos, mask[s][:, :].bitcast(U16), scan[s]))
                loop.end(NB // 2)
                a, b = scan[0].bitcast(I32), scan[1].bitcast(I32)
                r = row_at[d][:, :]
                gs = T * GT
                step(v.tensor_scalar(a, pos, -1.0, None, ALU.add))
                step(v.tensor_scalar(b, a, T - 1, GT.bit_length() - 1, ALU.bitwise_and, ALU.logical_shift_left))
                step(v.tensor_scalar(r, a, ~(gs - 1), None, ALU.bitwise_and))
                step(v.tensor_tensor(r, r, b, ALU.add))
                step(v.tensor_scalar(a, a, T.bit_length() - 1, GT - 1, ALU.arith_shift_right, ALU.bitwise_and))
                v.tensor_tensor(r, r, a, ALU.add).then_inc(s_row_at, 1)
            step(v.memset(stat[:, 0, 0:1], 0.0))

            def degree_onehots(s, cols):
                v.tensor_tensor(deg_p[s], lane[0:P, :].unsqueeze(1).to_broadcast([P, SC, P]),
                                part[SRC][:, cols].unsqueeze(2).to_broadcast([P, SC, P]), ALU.is_equal)
                v.tensor_tensor(deg_b[s], lane[0:P, 0:NB].unsqueeze(1).to_broadcast([P, SC, NB]),
                                blk[SRC][:, cols].unsqueeze(2).to_broadcast([P, SC, NB]), ALU.is_equal).then_inc(s_degoh[s], 1)

            def one_round(i):
                for s in range(2):
                    wait_past(dve, s_degmm[s], i)
                    degree_onehots(s, ds(i * (2 * SC) + s * SC, SC))

            rounds(dve, HALF, one_round)
            dve.wait_ge(s_deg, 1)
            step(v.tensor_copy(dinv[:, :], pout[0:P, 0:NB]))
            step(v.memset(AGG[:, :], 0.0))
            dve.wait_ge(s_x, 16)
            v.engine_nop().then_inc(s_table_ready, 1)

            def blocks(a):
                return a.rearrange("p (b f) -> p b f", f=D)

            def per_node(a):
                return a.unsqueeze(2).to_broadcast([P, NB, D])

            X3, A3, H3, T3 = blocks(X[:, :]), blocks(AGG[:, :]), blocks(H), blocks(TMP[0:P, :])
            sqrts = 0

            def inverse_root(values, root):
                nonlocal sqrts
                sqrts += 1
                v.engine_nop().then_inc(s_var, 1)
                dve.wait_ge(s_std, sqrts)
                step(v.reciprocal(root, root))

            def layernorm():
                step(v.tensor_reduce(stat[:, 0, :], X3, AX.X, ALU.add))
                step(v.tensor_scalar(stat[:, 0, :], stat[:, 0, :], 1.0 / D, None, ALU.mult))
                step(v.tensor_tensor(X3, X3, per_node(stat[:, 0, :]), ALU.subtract))
                step(v.tensor_tensor(T3, X3, X3, ALU.mult))
                step(v.tensor_reduce(stat[:, 1, :], T3, AX.X, ALU.add))
                step(v.tensor_scalar(stat[:, 1, :], stat[:, 1, :], 1.0 / D, EPS, ALU.mult, ALU.add))
                inverse_root(stat[:, 1, :], stat[:, 2, :])
                step(v.tensor_tensor(X3, X3, per_node(stat[:, 2, :]), ALU.mult))

            def transform(t, relu, target):
                def one_round(i):
                    o = target[:, ds(i * (QB * D), QB * D)]
                    dve.wait_ge(s_mm, i + (t * QUADS + 1))
                    v.tensor_tensor(blocks(o), blocks(pout[0:P, 0:QB * D]),
                                        bias[:, t, :].unsqueeze(1).to_broadcast([P, QB, D]), ALU.add).then_inc(s_mmu, 1)

                rounds(dve, QUADS, one_round)
                dve.wait_ge(s_mmu, (t + 1) * QUADS)
                if relu:
                    step(v.tensor_scalar(target, target, 0.0, None, ALU.max))

            for q, (d, kind) in enumerate(PASSES):
                if q == 1:
                    dve.wait_ge(s_back, 16)
                    step(v.tensor_copy(lo[SRC][:, :].unsqueeze(2),
                                       raw_back[:, :, :, :].rearrange("p g j c -> p (g j) c")[:, :, 1:2]))

                def onehots(i, s):
                    if kind == "edge":
                        dve.wait_ge(s_idx[q][s], i + 1)
                    v.tensor_tensor(onehot[s], lane[:, :].unsqueeze(1).to_broadcast([128, GT, P]),
                                    lo[d][:, ds(i * (2 * GT) + s * GT, GT)].unsqueeze(2).to_broadcast([128, GT, P]),
                                    ALU.is_equal).then_inc(s_oh[q][s], 1)

                def messages(i, s, link):
                    if kind == "edge":
                        dve.wait_ge(s_gath[q][s], i * (16 * GT) + 16 * GT)
                        link(v.tensor_tensor(msg[s][:, :, :], msg[s][:, :, :], rows[s][:, :, 0:D], ALU.add))
                        v.tensor_scalar(msg[s][:, :, :], msg[s][:, :, :], 0.0, None, ALU.max).then_inc(s_msg[q][s], 1)
                    elif kind == "weight":
                        dve.wait_ge(s_gath[q][s], i * (16 * GT) + 16 * GT)
                        v.tensor_tensor(msg[s][:, :, :], msg[s][:, :, :],
                                        w_s[:, ds(i * (2 * GT) + s * GT, GT)].unsqueeze(2).to_broadcast([128, GT, D]),
                                        ALU.mult).then_inc(s_msg[q][s], 1)

                def add_sums(i, s, link):
                    dve.wait_ge(s_sum[q][s], i + 1)
                    for j in range(GT):
                        h, k = divmod(j, GT // 2)
                        b = dve.value_load(tile_block[d][0:1, ds(i * (2 * GT) + (s * GT + j), 1)], min_val=0, max_val=NB - 1)
                        o = AGG[:, ds(b * D, D)]
                        m = v.tensor_tensor(o, o, pacc[s][0:P, h, k * D:(k + 1) * D], ALU.add)
                        if j < GT - 1:
                            link(m)
                    m.then_inc(s_added[q][s], 1)
                    dve.wait_ge(s_added[q][s], i + 1)

                for s in range(2):
                    onehots(0, s)
                    messages(0, s, step)
                with dve.Fori(1, PAIRS) as i:
                    loop = Loop(i, 1, 2 * (GT - 1 + (kind == "edge")))
                    for s in range(2):
                        add_sums(i - 1, s, loop.step)
                        onehots(i, s)
                        messages(i, s, loop.step)
                loop.end(PAIRS - 1)
                for s in range(2):
                    add_sums(PAIRS - 1, s, step)

                if q == 0:
                    dve.wait_ge(s_small, 16 * 9)
                    dve.wait_ge(s_table, 16)
                    step(v.tensor_scalar(eps_sb[:, :], eps_sb[:, :], 1.0, None, ALU.add))
                    step(v.scalar_tensor_tensor(AGG[:, :], X[:, :], eps_sb[:, 0:1], AGG[:, :], ALU.mult, ALU.add))
                    step(v.tensor_tensor(X[:, :], X[:, :], AGG[:, :], ALU.add))
                    layernorm()
                    inverse_root(dinv[:, :], dinv[:, :])
                    step(v.tensor_tensor(H3, X3, per_node(dinv[:, :]), ALU.mult))
                elif q in (1, 2):
                    dve.wait_ge(s_table, 16 * (q + 1))
                    step(v.tensor_tensor(H, H, AGG[:, :], ALU.add))
                    step(v.tensor_tensor(H3, H3, per_node(dinv[:, :]), ALU.mult))
                    if q == 1:
                        step(v.tensor_tensor(H3, H3, per_node(dinv[:, :]), ALU.mult))
                    else:
                        step(v.tensor_tensor(X[:, :], X[:, :], H, ALU.add))
                        layernorm()
                elif q == 3:
                    v.engine_nop().then_inc(s_node, 1)
                    dve.wait_ge(s_table, 16 * (q + 1))
                    transform(0, True, H)
                elif q == 4:
                    v.engine_nop().then_inc(s_node, 1)
                    dve.wait_ge(s_table, 16 * (q + 1))
                    transform(1, False, TMP[0:P, :])
                    step(v.tensor_tensor(X[:, :], X[:, :], TMP[0:P, :], ALU.add))
                    layernorm()
                else:
                    v.engine_nop().then_inc(s_node, 1)
                    dve.wait_ge(s_table, 16 * (q + 1))
                    transform(2, True, TMP[0:P, :])
                    step(v.tensor_tensor(X[:, :], X[:, :], TMP[0:P, :], ALU.add))
                    layernorm()
                    v.engine_nop().then_inc(s_res, 1)
                if q < len(PASSES) - 1:
                    step(v.memset(AGG[:, :], 0.0))
                    v.engine_nop().then_inc(s_table_ready, 1)


_INS = ["x", "src", "dst", "edge_attr_48", "edge_weight", "L0_gnn_eps", "L2_gnn_w_rel1", "L2_gnn_w_root1",
        "L2_gnn_b1", "L2_gnn_w_rel2", "L2_gnn_w_root2", "L2_gnn_b2", "L3_gnn_w", "L3_gnn_b"]


def kernel(**inputs):
    import numpy as _np
    import concourse.bacc as _bacc
    from concourse import mybir as _mybir
    from concourse.bass_utils import run_bass_kernel_spmd as _run

    nc = _bacc.Bacc("TRN2", target_bir_lowering=False, num_devices=1)
    arrays, args = {}, []
    for name in _INS:
        a = _np.ascontiguousarray(inputs[name])
        arrays[f"in_{name}_dram"] = a
        args.append(nc.dram_tensor(f"in_{name}_dram", a.shape, _mybir.dt.from_np(a.dtype), kind="ExternalInput").ap())
    args.append(nc.dram_tensor("out_0_dram", (N, D), F32, kind="ExternalOutput").ap())
    gnn_program(nc, *args)
    r = _run(nc, [arrays], core_ids=[0])
    return r.results[0]["out_0_dram"]
```

```python
import concourse.bass as bass
from concourse import mybir
from contextlib import ExitStack

F32 = mybir.dt.float32
BF16 = mybir.dt.bfloat16
I32 = mybir.dt.int32
U8 = mybir.dt.uint8
ALU = mybir.AluOpType
ACT = mybir.ActivationFunctionType
AX = mybir.AxisListType

N, E, D = 12500, 212500, 48
P = 125
NB = N // P
EC = E // P
K = 8
T = 128
GB = 4
CELLS = NB * NB
UNITS_MOST = (E + (K - 1) * CELLS) // K
BATCHES = 2 * GB * -(-((UNITS_MOST + (T - 1) * NB) // T) // (2 * GB))
U = BATCHES * T
ROW = D + 4
META = K + 1
NOBODY = 255
RC = 4
RS = 5
CC = 17
TC = 100
QB = 4
EPS = 1e-5
W3 = 3 * D
DST, SRC = 0, 1
PASSES = [(DST, "edge"), (SRC, "plain"), (SRC, "plain"), (DST, "plain"), (DST, "plain"), (DST, "weight")]


def rounds(engine, n, body):
    body(0)
    with engine.Fori(1, n) as i:
        body(i)


def wait_past(engine, semaphore, count):
    if not isinstance(count, int) or count > 0:
        engine.wait_ge(semaphore, count)


def load_blocks(engine, registers, numbers):
    engine.load(registers, numbers)
    return [engine.snap(r, min_val=0, max_val=NB - 1) for r in registers]


def gnn_program(nc, x_in, src_in, dst_in, ea_in, w_in, eps_in, w_rel1, w_root1, b1, w_rel2, w_root2, b2,
                w3, b3, out):
    assert NB * P == N and EC * P == E and EC % (RC * RS) == 0 and EC % (2 * CC) == 0 and EC % TC == 0
    assert NB % QB == 0 and BATCHES <= 512
    ds = bass.ds
    with ExitStack() as ctx:
        def sb(name, shape, dt=F32):
            return ctx.enter_context(nc.sbuf_tensor(name, shape, dt))

        def ps(name, shape):
            return ctx.enter_context(nc.psum_tensor(name, shape, F32))

        def sem(name):
            return ctx.enter_context(nc.semaphore(name))

        rows_dram = nc.dram_tensor("edge_rows", (U * K, ROW), F32).ap()
        meta_dram = nc.dram_tensor("unit_rows", (2 * U, META), F32).ap()
        shift_dram = nc.dram_tensor("cell_shift", (CELLS + 1, 1), F32).ap()
        block_dram = [nc.dram_tensor(f"blocks_by_edge{k}", (EC, P), BF16).ap() for k in range(2)]
        part_dram = [nc.dram_tensor(f"parts_by_slot{k}", (BATCHES, T * K), U8).ap() for k in range(2)]
        unit_dram = nc.dram_tensor("messages", (U, K * D), F32).ap()
        unit3_dram = nc.dram_tensor("messages_in_parts", (U, K * W3), BF16).ap()

        ones = sb("ones", [128, 128])
        before = sb("before", [128, 128])
        ident = sb("ident", [128, 128])
        ident_b = sb("ident_b", [128, 128], BF16)
        later = sb("later", [128, 128], BF16)
        lane = sb("lane", [128, P])
        here = sb("here", [128, 1])
        minus1 = sb("minus1", [128, 1])
        X = sb("X", [P, NB * D])
        AGG = sb("AGG", [P, NB * D])
        TMP = sb("TMP", [128, NB * D])
        EDGE = sb("EDGE", [P, 4 * EC])
        H = EDGE[:, 0:NB * D]
        V3_WORDS = sb("V3", [128, NB * W3 // 2])
        V3 = V3_WORDS[0:P, :].bitcast(BF16)
        stat = sb("stat", [P, 4, NB])
        dinv = sb("dinv", [P, NB])
        eps_sb = sb("eps_sb", [P, 1])
        bias = sb("bias", [P, 3, D])
        weights = sb("weights", [D, 5, D])
        edge = EDGE[:, :].rearrange("p (c k) -> p c k", k=4)
        field = {"src_part": edge[:, :, 0], "dst_part": edge[:, :, 1], "weight": edge[:, :, 2], "cell": edge[:, :, 3]}
        part = [field["dst_part"], field["src_part"]]
        node_i = [AGG[:, 0:EC].bitcast(I32), AGG[:, EC:2 * EC].bitcast(I32)]
        w_load = TMP[0:P, 0:EC]
        q_i, q_f, r_f, c_f = (TMP[0:P, EC:2 * EC].bitcast(I32), TMP[0:P, EC:2 * EC], TMP[0:P, 2 * EC:NB * D],
                              AGG[:, 2 * EC:NB * D])
        blk = [sb(f"blk{k}", [P, EC], BF16) for k in range(2)]
        count = sb("count", [NB, NB])
        units_i = sb("units_i", [NB, NB], I32)
        units = sb("units", [NB, NB])
        run = sb("run", [NB, NB])
        first = [sb(f"first{k}", [NB, NB]) for k in range(2)]
        place = sb("place", [NB, NB])
        tot_i = sb("tot_i", [NB, 1], I32)
        tot = sb("tot", [NB, 1])
        start = sb("start", [NB, 1])
        batch_no = sb("batch_no", [NB, BATCHES])
        begun = sb("begun", [NB, BATCHES])
        zero1 = sb("zero1", [1, 1])
        dzero = sb("dzero", [NB, NB])
        batch_block = [sb(f"batch_block{k}", [1, BATCHES], I32) for k in range(2)]
        slot_part = [sb(f"slot_part{k}", [128, BATCHES, K], BF16) for k in range(2)]
        w_s = sb("w_s", [128, BATCHES, K])
        source = [sb(f"source{k}", [128, BATCHES], I32) for k in range(2)]
        unit_meta = V3_WORDS[:, 0:BATCHES * META].rearrange("p (t c) -> p t c", c=META)
        u_cell, u_shift, u_here = (V3_WORDS[:, BATCHES * (META + k):BATCHES * (META + k + 1)] for k in range(3))
        filling = V3_WORDS[:, BATCHES * (META + 3):BATCHES * (META + 3) + K * ROW].rearrange("p (k c) -> p k c", c=ROW)
        WORK_N = 12200
        WORK = sb("WORK", [128, WORK_N])
        used = [0]

        def carve(parts, shape, dt=F32):
            n = 1
            for k in shape:
                n *= k
            words = -(-n * {F32: 4, I32: 4, BF16: 2, U8: 1}[dt] // 4)
            a = WORK[0:parts, used[0]:used[0] + words]
            used[0] += words
            assert used[0] <= WORK_N, used[0]
            if dt != F32:
                a = a.bitcast(dt)
            a = a[:, 0:n]
            if len(shape) == 2:
                a = a.rearrange("p (a b) -> p a b", b=shape[1])
            if len(shape) == 3:
                a = a.rearrange("p (a b c) -> p a b c", b=shape[1], c=shape[2])
            return a

        oh_count = [[carve(P, [CC, NB], BF16) for _ in range(2)] for _ in range(2)]
        turned = [carve(TC, [EC // TC, P], BF16) for k in range(2)]
        blk_f = carve(P, [EC])
        used[0] = 0
        row_buf = [carve(P, [RC, ROW]) for _ in range(RS)]
        at_stage = [carve(P, [RC], I32) for _ in range(RS)]
        rank = [carve(P, [RC]) for _ in range(RS)]
        seen = [carve(P, [RC]) for _ in range(RS)]
        blk_row = [[carve(NB, [RC * P], BF16) for _ in range(RS)] for _ in range(2)]
        ohT = [[carve(NB, [RC * P], BF16) for _ in range(RS)] for _ in range(2)]
        ohT_f = [carve(NB, [RC * P]) for _ in range(RS)]
        oh = [[TMP[0:P, (k * RS + g) * RC * NB // 2:(k * RS + g + 1) * RC * NB // 2].bitcast(BF16)
               .rearrange("p (a b) -> p a b", b=NB) for g in range(RS)] for k in range(2)]
        picked = TMP[0:P, RS * RC * NB:RS * RC * NB + RC * NB].rearrange("p (a b) -> p a b", b=NB)
        junk = TMP[0:P, RS * RC * NB + RC * NB:RS * RC * NB + RC * NB + RC * P]
        TMPB = TMP[:, :].bitcast(BF16)
        deg_p = [TMPB[0:P, k * CC * P:(k + 1) * CC * P].rearrange("p (c m) -> p c m", m=P) for k in range(2)]
        deg_b = [TMPB[0:P, 2 * CC * P + k * CC * NB:2 * CC * P + (k + 1) * CC * NB]
                 .rearrange("p (c m) -> p c m", m=NB) for k in range(2)]
        used[0] = 0
        rows = [carve(128, [GB, K, ROW]) for _ in range(2)]
        idx = [carve(128, [GB], I32) for _ in range(2)]
        got = [carve(128, [GB]) for _ in range(2)]
        msg3 = [carve(128, [GB, K * W3], BF16) for _ in range(2)]
        msg = [m.rearrange("p a b -> p (a b)").bitcast(F32)[:, 0:GB * K * D].rearrange("p (a b) -> p a b", b=K * D)
               for m in msg3]
        cut = [carve(128, [K, W3], BF16) for _ in range(2)]
        meta_buf = [m[:, 0, 0:GB * META].rearrange("p (a b) -> p a b", b=META) for m in msg]
        part_row = [carve(P, [GB, T * K], U8) for _ in range(2)]
        SEL = [carve(128, [T * K], BF16) for _ in range(2)]
        select = [s[0:P, :].rearrange("p (u k) -> p k u", k=K) for s in SEL]
        onehot = [s[:, 0:K * P].rearrange("p (k m) -> p k m", m=P) for s in SEL]
        part_out = TMP[:, 0:BATCHES * K // 4].bitcast(U8)
        pair_sum = [TMP[0:P, k * 2 * D:(k + 1) * 2 * D].rearrange("p (a f) -> p a f", f=D) for k in range(2)]
        target = TMP[:, 1000:1000 + BATCHES]
        target_i = TMP[:, 1400:1400 + BATCHES].bitcast(I32)
        valid = TMP[:, 1800:1800 + BATCHES]
        used[0] = 0
        quad = [carve(P, [QB * D]) for k in range(2)]
        tT = [carve(D, [QB * P]) for k in range(2)]

        bank = [ps(f"bank{k}", [128, 512]) for k in range(8)]

        s_edges, s_x, s_small, s_const = sem("edges_loaded"), sem("x_loaded"), sem("small_loaded"), sem("constants_ready")
        s_fill, s_filled = sem("fill_ready"), sem("dram_filled")
        s_pool_turn, s_pe_turn, s_sp_turn = sem("gpsimd_turn"), sem("tensor_turn"), sem("sync_turn")
        s_dve = sem("vector_step")
        s_coh, s_cmm, s_cnt = sem("count_onehots_ready"), sem("count_onehots_used"), sem("cells_counted")
        s_blkf, s_turn, s_turned, s_blkdram = (sem("blocks_ready"), sem("blocks_turned"), sem("turned_copied"),
                                               sem("blocks_written"))
        s_tab, s_tabmm = sem("table_operand_ready"), sem("table_product_ready")
        s_shift, s_shiftw = sem("shifts_ready"), sem("shifts_written")
        s_load = [sem(f"rank_inputs_loaded{g}") for g in range(RS)]
        s_roh, s_rf, s_look = sem("rank_onehots_ready"), sem("rank_onehots_widened"), sem("cells_looked_up")
        s_eq, s_rank, s_fin = sem("equal_cells_found"), sem("ranks_summed"), sem("places_moved_on")
        s_meta, s_at = sem("edge_fields_staged"), sem("edge_slots_ready")
        s_scat = [sem(f"edges_scattered{g}") for g in range(RS)]
        s_doh, s_dmm, s_deg = sem("degree_onehots_ready"), sem("degree_onehots_used"), sem("degrees_summed")
        s_rows = [sem(f"rows_loaded{s}") for s in range(2)]
        s_rowsu = sem("rows_used")
        s_cell, s_got, s_gotu = sem("cells_staged"), [sem(f"shifts_gathered{s}") for s in range(2)], sem("shifts_copied")
        s_target = sem("unit_targets_ready")
        s_mst, s_mscat = sem("unit_rows_staged"), [sem(f"unit_rows_scattered{s}") for s in range(2)]
        s_mback, s_pout, s_pdram = sem("unit_rows_loaded"), sem("slot_parts_ready"), sem("slot_parts_written")
        s_value = sem("node_values_ready")
        s_prow = [sem(f"part_rows_loaded{s}") for s in range(2)]
        s_sel, s_spread, s_stage = sem("selectors_ready"), sem("messages_selected"), sem("messages_staged")
        s_reduced = sem("pair_sums_reduced")
        s_stage3, s_relu, s_high, s_rest, s_mid, s_cut = (sem("middle_slots_staged"), sem("messages_rectified"), sem("high_parts_cut"),
                                                  sem("rests_ready"), sem("middle_parts_cut"), sem("messages_cut"))
        s_store = [sem(f"messages_stored{s}") for s in range(2)]
        s_idx, s_gath = sem("unit_indices_staged"), [sem(f"messages_gathered{s}") for s in range(2)]
        s_msg, s_oh, s_sum, s_added = sem("messages_ready"), sem("onehots_ready"), sem("batches_summed"), sem("sums_added")
        s_var, s_std = sem("variance_ready"), sem("deviation_ready")
        s_node, s_quad, s_tr, s_trc = sem("aggregate_ready"), sem("blocks_staged"), sem("blocks_transposed"), sem("transposes_copied")
        s_mm, s_mmu, s_res, s_out = sem("blocks_multiplied"), sem("products_used"), sem("result_ready"), sem("output_written")

        TURNS = EC // (RC * RS)
        COUNTS = EC // (2 * CC)
        PAIRS = BATCHES // (2 * GB)
        GROUPS = BATCHES // GB
        QUADS = NB // QB
        rows_v = rows_dram.rearrange("(t p k) c -> p t (k c)", p=128, k=K)
        meta_v = meta_dram[0:U, :].rearrange("(t p) c -> p t c", p=128)
        unit3_v = unit3_dram.rearrange("(t p) c -> p t c", p=128)
        unit_v = unit_dram.rearrange("(t p) c -> p t c", p=128)
        ea_c = ea_in.rearrange("(p c) f -> p c f", p=P)
        TRANSFORMS = [(0, 1), (2, 3), (4, None)]

        def sum_bank(j):
            return bank[6 + j // 2 % 2][0:P, j % 2 * W3:(j % 2 + 1) * W3]

        def spread_bank(j, k):
            return bank[3 * (j % 2) + k // 3]

        def plain_before(q):
            return BATCHES * sum(kind == "plain" for _, kind in PASSES[:q])

        def cut_before(q):
            return BATCHES * q - plain_before(q)

        block = ctx.enter_context(nc.Block())

        @block.sync
        def _(sp):
            sp.dma_start(node_i[DST], dst_in.rearrange("(p c) -> p c", p=P)).then_inc(s_edges, 16)
            sp.dma_start(node_i[SRC], src_in.rearrange("(p c) -> p c", p=P)).then_inc(s_edges, 16)
            sp.dma_start(w_load, w_in.rearrange("(p c) -> p c", p=P)).then_inc(s_edges, 16)
            sp.wait_ge(s_fill, 1)
            sp.dma_start(rows_v, filling.rearrange("p k c -> p (k c)").unsqueeze(1)
                         .to_broadcast([128, BATCHES, K * ROW])).then_inc(s_filled, 16)
            sp.dma_start(meta_v, unit_meta[:, 0:1, :].to_broadcast([128, BATCHES, META])).then_inc(s_filled, 16)
            sp.dma_start(shift_dram[CELLS:CELLS + 1, :], zero1[:, :]).then_inc(s_filled, 16)
            sp.dma_start(X[:, :], x_in.rearrange("(p b) f -> p (b f)", p=P)).then_inc(s_x, 16)
            for k, w in enumerate((w_rel1, w_root1, w_rel2, w_root2, w3)):
                sp.dma_start(weights[:, k, :], w).then_inc(s_small, 16)
            for k, b in enumerate((b1, b2, b3)):
                sp.dma_start(bias[:, k, :], b.rearrange("(a n) -> a n", a=1).to_broadcast([P, D])).then_inc(s_small, 16)
            sp.dma_start(eps_sb[:, :], eps_in.rearrange("(a n) -> a n", a=1).to_broadcast([P, 1])).then_inc(s_small, 16)
            sp.wait_ge(s_turned, 2 * (EC // TC))
            for k in range(2):
                sp.dma_start(block_dram[k].rearrange("(a c) p -> c a p", c=TC), turned[k]).then_inc(s_blkdram, 16)
            sp.wait_ge(s_blkdram, 32)
            sp.wait_ge(s_shift, 1)
            sp.dma_start(shift_dram[0:CELLS, :].rearrange("(a b) o -> a (b o)", b=NB), run[:, :]).then_inc(s_shiftw, 16)

            def load_columns(i):
                for g in range(RS):
                    n = i * RS + g
                    wait_past(sp, s_scat[g], i * (16 * RC))
                    sp.sem_inc(s_sp_turn, 1)
                    wait_past(sp, s_roh, n - (RS - 1))
                    sp.sem_inc(s_sp_turn, 1)
                    sp.dma_start(row_buf[g][:, :, 0:D], ea_c[:, ds(n * RC, RC), :]).then_inc(s_load[g], 16)
                    for k in range(2):
                        sp.dma_start(blk_row[k][g], block_dram[k][ds(n * RC, RC), :].rearrange("c p -> (c p)")
                                     .unsqueeze(0).to_broadcast([NB, RC * P])).then_inc(s_load[g], 16)

            rounds(sp, TURNS, load_columns)

            def load_rows(i, base):
                for s in range(2):
                    wait_past(sp, s_rowsu, i * 2 + (base + s - 1))
                    sp.sem_inc(s_sp_turn, 1)
                    sp.dma_start(rows[s].rearrange("p t k c -> p t (k c)"),
                                 rows_v[:, ds(i * (2 * GB) + s * GB, GB), :]).then_inc(s_rows[s], 16)

            for g in range(RS):
                sp.wait_ge(s_scat[g], TURNS * 16 * RC)
            rounds(sp, PAIRS, lambda i: load_rows(i, 0))
            sp.wait_ge(s_pout, 1)
            sp.dma_start(part_dram[DST].rearrange("t (p k) -> p t k", k=K),
                         part_out.rearrange("p (t k) -> p t k", k=K)).then_inc(s_pdram, 16)
            for s in range(2):
                sp.wait_ge(s_mscat[s], PAIRS * 16 * GB)
            sp.dma_start(unit_meta[:, :, :], meta_v).then_inc(s_mback, 16)
            sp.wait_ge(s_pout, 2)
            sp.dma_start(part_dram[SRC].rearrange("t (p k) -> p t k", k=K),
                         part_out.rearrange("p (t k) -> p t k", k=K)).then_inc(s_pdram, 16)
            sp.wait_ge(s_pdram, 32)
            for q, (d, kind) in enumerate(PASSES):
                def load_parts(i):
                    for s in range(2):
                        wait_past(sp, s_sel, (i * 2 + s - 1) * GB + q * BATCHES)
                        sp.sem_inc(s_sp_turn, 1)
                        sp.dma_start(part_row[s].rearrange("p a b -> p (a b)"),
                                     part_dram[1 - d][ds(i * (2 * GB) + s * GB, GB), :].rearrange("t n -> (t n)")
                                     .unsqueeze(0).to_broadcast([P, GB * T * K])).then_inc(s_prow[s], 16)

                rounds(sp, PAIRS, load_parts)
                if kind == "edge":
                    rounds(sp, PAIRS, lambda i: load_rows(i, 2 * PAIRS))
            sp.wait_ge(s_res, 1)
            sp.dma_start(out.rearrange("(p b) f -> p (b f)", p=P), X[:, :]).then_inc(s_out, 16)
            sp.wait_ge(s_out, 16)

        @block.gpsimd
        def _(pool):
            pool.memset(ones[:, :], 1.0).then_inc(s_const, 1)
            pool.memset(minus1[:, :], -1.0).then_inc(s_const, 1)
            pool.iota(lane[:, :], [[1, P]], base=0, channel_multiplier=0,
                      allow_small_or_imprecise_dtypes=True).then_inc(s_const, 1)
            pool.iota(here[:, :], [[1, 1]], base=0, channel_multiplier=1,
                      allow_small_or_imprecise_dtypes=True).then_inc(s_const, 1)
            pool.iota(batch_no[:, :], [[1, BATCHES]], base=0, channel_multiplier=0,
                      allow_small_or_imprecise_dtypes=True).then_inc(s_const, 1)
            pool.iota(u_here[:, :], [[T, BATCHES]], base=0, channel_multiplier=1,
                      allow_small_or_imprecise_dtypes=True).then_inc(s_const, 1)
            pool.memset(before[:, :], 1.0).then_inc(s_const, 1)
            pool.memset(ident[:, :], 1.0).then_inc(s_const, 1)
            pool.memset(ident_b[:, :], 1.0).then_inc(s_const, 1)
            pool.memset(later[:, :], 0.0).then_inc(s_const, 1)
            pool.wait_ge(s_const, 10)
            pool.affine_select(out=before[:, :], in_=before[:, :], compare_op=ALU.is_gt, fill=0.0, base=0,
                               pattern=[[1, 128]], channel_multiplier=-1).then_inc(s_const, 1)
            for m in (ident, ident_b):
                pool.affine_select(out=m[:, :], in_=m[:, :], compare_op=ALU.is_equal, fill=0.0, base=0,
                                   pattern=[[1, 128]], channel_multiplier=-1).then_inc(s_const, 1)
            pool.affine_select(out=later[:, :], in_=later[:, :], compare_op=ALU.is_gt, fill=-1024.0, base=0,
                               pattern=[[-1, 128]], channel_multiplier=1).then_inc(s_const, 1)

            def scatter_rows(i):
                for g in range(RS):
                    pool.wait_ge(s_at, i * RS + (g + 1))
                    pool.wait_ge(s_meta, i * RS + (g + 1))
                    pool.wait_ge(s_load[g], i * 48 + 48)
                    pool.wait_ge(s_filled, 48)
                    pool.sem_inc(s_pool_turn, 1)
                    for j in range(RC):
                        pool.indirect_dma_start(
                            rows_dram, bass.IndirectOffsetOnAxis(ap=at_stage[g][:, j:j + 1], axis=0),
                            row_buf[g][:, j, :], None).then_inc(s_scat[g], 16)

            rounds(pool, TURNS, scatter_rows)

            def gather_shifts(i):
                for s in range(2):
                    pool.wait_ge(s_cell, i * 2 + (s + 1))
                    pool.wait_ge(s_shiftw, 16)
                    pool.sem_inc(s_pool_turn, 1)
                    for j in range(GB):
                        pool.indirect_dma_start(
                            got[s][:, j:j + 1], None, shift_dram,
                            bass.IndirectOffsetOnAxis(ap=idx[s][:, j:j + 1], axis=0)).then_inc(s_got[s], 16)

            rounds(pool, PAIRS, gather_shifts)

            def scatter_units(i):
                for s in range(2):
                    pool.wait_ge(s_mst, i * 2 + (s + 1))
                    pool.wait_ge(s_filled, 48)
                    pool.sem_inc(s_pool_turn, 1)
                    for j in range(GB):
                        pool.indirect_dma_start(
                            meta_dram, bass.IndirectOffsetOnAxis(ap=idx[s][:, j:j + 1], axis=0),
                            meta_buf[s][:, j, :], None).then_inc(s_mscat[s], 16)

            rounds(pool, PAIRS, scatter_units)
            for q, (d, kind) in enumerate(PASSES):
                def gather_group(i, s):
                    g = i * 2 + (q * GROUPS + s)
                    pool.wait_ge(s_idx, g + 1)
                    if not isinstance(i, int):
                        pool.wait_ge(s_sum, (i - 1) * (2 * GB) + (q * BATCHES + (s + 1) * GB))
                    for k in range(2):
                        pool.wait_ge(s_store[k], 16 * PAIRS * (q + 1))
                    pool.sem_inc(s_pool_turn, 1)
                    for j in range(GB):
                        pool.indirect_dma_start(
                            (msg3 if kind == "plain" else msg)[s][:, j, :], None,
                            unit3_dram if kind == "plain" else unit_dram,
                            bass.IndirectOffsetOnAxis(ap=idx[s][:, j:j + 1], axis=0)).then_inc(s_gath[s], 16)

                def take_low(i, s):
                    for j in range(GB):
                        m3 = msg[s][:, j, :].rearrange("p (k f) -> p k f", f=D)
                        pool.wait_ge(s_mid, i * (2 * GB) + (s * GB + j + 1 + cut_before(q)))
                        nc.gpsimd.tensor_tensor(cut[j % 2][:, :, 2 * D:W3], m3, cut[j % 2][:, :, D:2 * D],
                                                ALU.subtract).then_inc(s_cut, 1)

                def gather_units(i):
                    for s in range(2):
                        gather_group(i, s)
                        if kind != "plain" and s > 0:
                            take_low(i, 0)
                        elif kind != "plain" and not isinstance(i, int):
                            take_low(i - 1, 1)

                rounds(pool, PAIRS, gather_units)
                if kind != "plain":
                    take_low(PAIRS - 1, 1)

        @block.scalar
        def _(act):
            act.wait_ge(s_const, 14)
            for k in range(2):
                for c in range(EC // TC):
                    n = k * (EC // TC) + c
                    act.wait_ge(s_turn, n + 1)
                    act.copy(turned[k][:, c, :], bank[2 + n % 2][0:TC, 0:P]).then_inc(s_turned, 1)

            def sum_ranks(i, g):
                n = i * RS + g
                for j in range(RC):
                    act.wait_ge(s_eq, n * RC + (j + 1))
                    wait_past(act, s_rank, n * RC + j)
                    act.activation(junk[:, 0:(j + 1) * P], bank[2 + j % 2][0:P, 0:(j + 1) * P], ACT.Relu,
                                   bias=minus1[0:P, :], accum_out=rank[g][:, j:j + 1]).then_inc(s_rank, 1)

            def rank_edges(i):
                for g in range(RS):
                    n = i * RS + g
                    act.wait_ge(s_roh, n + 1)
                    wait_past(act, s_look, n - (RS - 1))
                    act.copy(ohT_f[g], ohT[DST][g]).then_inc(s_rf, 1)
                    wait_past(act, s_scat[g], i * (16 * RC))
                    act.copy(row_buf[g][:, :, D:ROW], edge[:, ds(n * RC, RC), :]).then_inc(s_meta, 1)
                    if g > 0:
                        sum_ranks(i, g - 1)
                    elif not isinstance(i, int):
                        sum_ranks(i - 1, RS - 1)

            act.wait_ge(s_blkdram, 32)
            rounds(act, TURNS, rank_edges)
            sum_ranks(TURNS - 1, RS - 1)

            def copy_shifts(i, s):
                act.wait_ge(s_got[s], (i + 1) * (16 * GB))
                act.copy(u_shift[:, ds(i * (2 * GB) + s * GB, GB)], got[s]).then_inc(s_gotu, 1)

            def take_fields(i):
                for s in range(2):
                    if not isinstance(i, int):
                        copy_shifts(i - 1, s)
                    cols = ds(i * (2 * GB) + s * GB, GB)
                    act.wait_ge(s_rows[s], i * 16 + 16)
                    act.copy(idx[s].unsqueeze(2), rows[s][:, :, 0, D + 3:D + 4])
                    act.copy(u_cell[:, cols].unsqueeze(2), rows[s][:, :, 0, D + 3:D + 4]).then_inc(s_cell, 1)
                    act.copy(unit_meta[:, cols, 0:K], rows[s][:, :, :, D])
                    act.copy(slot_part[DST][:, cols, :], rows[s][:, :, :, D + 1])
                    act.copy(w_s[:, cols, :], rows[s][:, :, :, D + 2]).then_inc(s_rowsu, 1)

            act.wait_ge(s_filled, 48)
            rounds(act, PAIRS, take_fields)
            for s in range(2):
                copy_shifts(PAIRS - 1, s)

            act.wait_ge(s_target, 1)

            def stage_units(i):
                for s in range(2):
                    cols = ds(i * (2 * GB) + s * GB, GB)
                    wait_past(act, s_mscat[s], i * (16 * GB))
                    act.copy(idx[s], target_i[:, cols])
                    act.copy(meta_buf[s], unit_meta[:, cols, :]).then_inc(s_mst, 1)

            rounds(act, PAIRS, stage_units)
            for s in range(2):
                act.wait_ge(s_mscat[s], PAIRS * 16 * GB)
            act.wait_ge(s_mback, 16)

            sqrts = [0]

            def sqrt(out_, in_):
                sqrts[0] += 1
                act.wait_ge(s_var, sqrts[0])
                act.activation(out_, in_, ACT.Sqrt).then_inc(s_std, 1)

            def copy_transposes(t):
                own = TRANSFORMS[t][1] is not None
                act.wait_ge(s_node, t + 1)

                def one_round(i):
                    n = i + t * QUADS
                    wait_past(act, s_tr, n)
                    cols = ds(i * (QB * D), QB * D)
                    if own:
                        act.copy(quad[1], (X[:, :], H)[t][:, cols])
                    act.copy(quad[0], AGG[:, cols]).then_inc(s_quad, 1)
                    act.wait_ge(s_tr, n + 1)
                    wait_past(act, s_mm, n)
                    if own:
                        act.copy(tT[1], bank[1][0:D, 0:QB * P])
                    act.copy(tT[0], bank[0][0:D, 0:QB * P]).then_inc(s_trc, 1)

                rounds(act, QUADS, one_round)

            for q, (d, kind) in enumerate(PASSES):
                def stage_messages(i):
                    for s in range(2):
                        if q == 0:
                            wait_past(act, s_store[s], i * 16)
                        elif isinstance(i, int):
                            act.wait_ge(s_sum, q * BATCHES)
                        else:
                            act.wait_ge(s_store[s], i * 16 + 16 * PAIRS * q)
                        for j in range(GB):
                            n = (i * 2 + s) * GB + (q * BATCHES + j)
                            act.wait_ge(s_spread, n + 1)
                            if kind == "plain":
                                for k in (0, 6):
                                    w = min(3, K - k) * W3
                                    m = act.copy(msg3[s][:, j, k * W3:k * W3 + w], spread_bank(j, k)[:, 0:w])
                            else:
                                m = act.copy(msg[s][:, j, :], bank[j % 2][:, 0:K * D])
                            m.then_inc(s_stage, 1)
                        act.wait_ge(s_stage, (i * 2 + s + 1) * GB + q * BATCHES)
                        to = ds(i * (2 * GB) + s * GB, GB)
                        if kind == "plain":
                            act.wait_ge(s_stage3, (i * 2 + s + 1) * GB + plain_before(q))
                            act.dma_start(unit3_v[:, to, :], msg3[s]).then_inc(s_store[s], 16)
                        else:
                            act.dma_start(unit_v[:, to, :], msg[s]).then_inc(s_store[s], 16)

                rounds(act, PAIRS, stage_messages)

                def cut_messages(i, s):
                    act.wait_ge(s_msg, i * 2 + ((0 if q == 0 else GROUPS) + s + 1))
                    for j in range(GB + 1):
                        t = i * (2 * GB) + (s * GB + j)
                        if j < GB:
                            m3 = msg[s][:, j, :].rearrange("p (k f) -> p k f", f=D)
                            if kind == "edge":
                                act.activation(msg[s][:, j, :], msg[s][:, j, :], ACT.Relu).then_inc(s_relu, 1)
                                act.wait_ge(s_relu, t + 1)
                            wait_past(act, s_sum, t + (q * BATCHES - 1))
                            act.copy(cut[j % 2][:, :, 0:D], m3).then_inc(s_high, 1)
                        if j > 0:
                            m3 = msg[s][:, j - 1, :].rearrange("p (k f) -> p k f", f=D)
                            act.wait_ge(s_rest, t + cut_before(q))
                            act.copy(cut[(j - 1) % 2][:, :, D:2 * D], m3).then_inc(s_mid, 1)

                def stage_indices(i):
                    for s in range(2):
                        if not isinstance(i, int) or q > 0:
                            act.wait_ge(s_gath[s], (i + q * PAIRS) * (16 * GB))
                        act.copy(idx[s], source[d][:, ds(i * (2 * GB) + s * GB, GB)]).then_inc(s_idx, 1)
                        if kind != "plain":
                            if s > 0:
                                cut_messages(i, 0)
                            elif not isinstance(i, int):
                                cut_messages(i - 1, 1)

                rounds(act, PAIRS, stage_indices)
                if kind != "plain":
                    cut_messages(PAIRS - 1, 1)
                if q == 0:
                    sqrt(stat[:, 2, :], stat[:, 1, :])
                    sqrt(dinv[:, :], dinv[:, :])
                if q == 2:
                    sqrt(stat[:, 2, :], stat[:, 1, :])
                if q >= 3:
                    copy_transposes(q - 3)
                if q >= 4:
                    sqrt(stat[:, 2, :], stat[:, 1, :])

        @block.tensor
        def _(pe):
            pe.wait_ge(s_const, 14)
            for k in range(2):
                pe.wait_ge(s_blkf, k + 1)
                for c in range(EC // TC):
                    n = k * (EC // TC) + c
                    if n >= 2:
                        pe.wait_ge(s_turned, n - 1)
                    pe.transpose(bank[2 + n % 2][0:TC, 0:P], blk_f[:, c * TC:(c + 1) * TC], ident[0:P, 0:P]).then_inc(s_turn, 1)

            def count_cells(i):
                for s in range(2):
                    pe.wait_ge(s_coh, i * 2 + (s + 1))
                    for c in range(CC):
                        m = pe.matmul(bank[0][0:NB, 0:NB], oh_count[s][0][:, c, :], oh_count[s][1][:, c, :],
                                      start=isinstance(i, int) and s == 0 and c == 0, stop=False)
                    m.then_inc(s_cmm, 1)

            rounds(pe, COUNTS, count_cells)
            pe.matmul(bank[0][0:NB, 0:NB], ident[0:NB, 0:NB], dzero[:, :], start=False, stop=True).then_inc(s_cnt, 1)
            tabs = [0]

            def product(out_, a, b, transpose=False):
                tabs[0] += 1
                pe.wait_ge(s_tab, tabs[0])
                (pe.transpose if transpose else lambda o, x, y: pe.matmul(o, x, y, start=True, stop=True))(out_, a, b)\
                    .then_inc(s_tabmm, 1)

            for o in (DST, SRC):
                if o == SRC:
                    product(bank[1][0:NB, 0:NB], count[:, :], ident[0:NB, 0:NB], True)
                product(bank[1][0:NB, 128:129], before[0:NB, 0:NB], tot[:, :])
                product(bank[7][0:1, 0:BATCHES], ones[0:NB, 0:1], begun[:, :])
            product(bank[1][0:NB, 0:NB], first[SRC][:, :], ident[0:NB, 0:NB], True)

            def rank_edges(i):
                for g in range(RS):
                    n = i * RS + g
                    pe.wait_ge(s_roh, n + 1)
                    wait_past(pe, s_fin, n)
                    for j in range(RC):
                        pe.matmul(bank[0][0:NB, 0:NB], oh[DST][g][:, j, :], oh[SRC][g][:, j, :], start=j == 0, stop=j == RC - 1)
                    pe.wait_ge(s_rf, n + 1)
                    for j in range(RC):
                        m = pe.matmul(bank[1][0:P, j * NB:(j + 1) * NB], ohT_f[g][:, j * P:(j + 1) * P], place[:, :],
                                      start=True, stop=True)
                    m.then_inc(s_look, 1)
                    for j in range(RC):
                        b = bank[2 + j % 2]
                        me, upto = slice(j * P, (j + 1) * P), slice(0, (j + 1) * P)
                        wait_past(pe, s_rank, n * RC + (j - 1))
                        pe.matmul(b[0:P, upto], ohT[DST][g][:, me], ohT[DST][g][:, upto], start=True, stop=False)
                        pe.matmul(b[0:P, me], ident_b[0:P, 0:P], later[0:P, 0:P], start=False, stop=False)
                        pe.matmul(b[0:P, upto], ohT[SRC][g][:, me], ohT[SRC][g][:, upto], start=False, stop=True).then_inc(s_eq, 1)

            rounds(pe, TURNS, rank_edges)

            def degrees(i):
                for s in range(2):
                    pe.wait_ge(s_doh, i * 2 + (s + 1))
                    for c in range(CC):
                        m = pe.matmul(bank[4][0:P, 0:NB], deg_p[s][:, c, :], deg_b[s][:, c, :],
                                      start=isinstance(i, int) and s == 0 and c == 0, stop=False)
                    m.then_inc(s_dmm, 1)

            rounds(pe, COUNTS, degrees)
            pe.matmul(bank[4][0:P, 0:NB], ones[0:1, 0:P], ones[0:1, 0:NB], start=False, stop=True).then_inc(s_deg, 1)

            def transform(t):
                rel, root = TRANSFORMS[t]
                pe.wait_ge(s_small, 16 * 9)

                def one_round(i):
                    n = i + t * QUADS
                    pe.wait_ge(s_quad, n + 1)
                    wait_past(pe, s_trc, n)
                    pe.sem_inc(s_pe_turn, 1)
                    for b in range(QB):
                        if root is not None:
                            pe.transpose(bank[1][0:D, b * P:(b + 1) * P], quad[1][:, b * D:(b + 1) * D], ident[0:P, 0:P])
                    for b in range(QB):
                        m = pe.transpose(bank[0][0:D, b * P:(b + 1) * P], quad[0][:, b * D:(b + 1) * D], ident[0:P, 0:P])
                    m.then_inc(s_tr, 1)
                    pe.wait_ge(s_trc, n + 1)
                    wait_past(pe, s_mmu, n)
                    for b in range(QB):
                        o = bank[4][0:P, b * D:(b + 1) * D]
                        m = pe.matmul(o, tT[0][:, b * P:(b + 1) * P], weights[:, rel, :], start=True, stop=root is None)
                        if root is not None:
                            m = pe.matmul(o, tT[1][:, b * P:(b + 1) * P], weights[:, root, :], start=False, stop=True)
                    m.then_inc(s_mm, 1)

                rounds(pe, QUADS, one_round)

            batch_regs = [pe.alloc_register(f"batch_block{k}") for k in range(2 * GB)]
            for q, (d, kind) in enumerate(PASSES):
                pe.wait_ge(s_value, q + 1)

                def select_rows(i):
                    its_block = load_blocks(pe, batch_regs, batch_block[1 - d][0:1, ds(i * (2 * GB), 2 * GB)])
                    for s in range(2):
                        for j in range(GB):
                            t = i * (2 * GB) + (s * GB + j)
                            n = t + q * BATCHES
                            b = its_block[s * GB + j]
                            pe.wait_ge(s_sel, n + 1)
                            wait_past(pe, s_stage, n - 1)
                            if kind == "plain":
                                wait_past(pe, s_stage3, t + (plain_before(q) - 1))
                            for k in range(K):
                                if kind == "plain":
                                    o = spread_bank(j, k)[:, k % 3 * W3:(k % 3 + 1) * W3]
                                    m = pe.matmul(o, select[j % 2][:, k, :], V3[:, ds(b * W3, W3)], start=True, stop=True)
                                    continue
                                for c in range(3):
                                    m = pe.matmul(bank[j % 2][:, k * D:(k + 1) * D], select[j % 2][:, k, :],
                                                  V3[:, ds(b * W3 + c * D, D)], start=c == 0, stop=c == 2)
                            m.then_inc(s_spread, 1)

                rounds(pe, PAIRS, select_rows)

                def sum_batches(i):
                    for s in range(2):
                        g = i * 2 + (q * GROUPS + s)
                        if kind == "plain":
                            pe.wait_ge(s_gath[s], (i + (q * PAIRS + 1)) * (16 * GB))
                        for j in range(GB):
                            n = i * (2 * GB) + (s * GB + j + q * BATCHES)
                            pe.wait_ge(s_oh, n + 1)
                            if kind != "plain":
                                pe.wait_ge(s_cut, i * (2 * GB) + (s * GB + j + 1 + cut_before(q)))
                            if j % 2 == 0:
                                wait_past(pe, s_reduced, i * GB + ((s * GB + j) // 2 + q * (BATCHES // 2) - 1))
                            for k in range(K):
                                parts = msg3[s][:, j, k * W3:(k + 1) * W3] if kind == "plain" else cut[j % 2][:, k, :]
                                m = pe.matmul(sum_bank(j), onehot[j % 2][:, k, :], parts,
                                              start=k == 0, stop=k == K - 1)
                            m.then_inc(s_sum, 1)

                rounds(pe, PAIRS, sum_batches)
                if q >= 3:
                    transform(q - 3)

        @block.vector
        def _(dve):
            v = nc.vector
            batch_regs = [dve.alloc_register(f"batch_block_v{k}") for k in range(2 * GB)]
            done = [0]

            def step(ins):
                done[0] += 1
                ins.then_inc(s_dve, 1)
                dve.wait_ge(s_dve, done[0])

            def stepped_rounds(n, steps, body):
                body(0, step)
                base = done[0]
                with dve.Fori(1, n) as i:
                    at = [0]

                    def mark(ins):
                        at[0] += 1
                        ins.then_inc(s_dve, 1)
                        dve.wait_ge(s_dve, i * steps + (base - steps + at[0]))

                    body(i, mark)
                    assert at[0] == steps, at[0]
                done[0] += (n - 1) * steps

            step(v.memset(filling, 0.0))
            step(v.memset(unit_meta[:, :, :], 0.0))
            v.memset(filling[:, :, D:D + 2], float(NOBODY))
            v.memset(filling[:, :, D + 3:D + 4], float(CELLS))
            v.memset(unit_meta[:, 0:1, 0:K], float(NOBODY))
            v.memset(dzero[:, :], 0.0)
            v.memset(zero1[:, :], 0.0).then_inc(s_fill, 1)
            dve.wait_ge(s_edges, 48)
            dve.wait_ge(s_const, 14)
            v.tensor_copy(field["weight"], w_load)
            for d in (SRC, DST):
                step(v.tensor_scalar(q_i, node_i[d], 1.0 / NB, 0.5 / NB - 0.5, ALU.mult, ALU.add))
                step(v.tensor_copy(part[d], q_i))
                for a, b in ((0, 1400), (1400, EC)):
                    p_, n_, w = part[d][:, a:b], node_i[d][:, a:b], b - a
                    r_, c_ = r_f[:, 0:w], c_f[:, 0:w]
                    step(v.scalar_tensor_tensor(r_, p_, -float(NB), n_, ALU.mult, ALU.add))
                    step(v.tensor_scalar(c_, r_, float(NB), None, ALU.is_ge))
                    step(v.tensor_tensor(p_, p_, c_, ALU.add))
                    step(v.scalar_tensor_tensor(r_, c_, -float(NB), r_, ALU.mult, ALU.add))
                    step(v.tensor_scalar(c_, r_, 0.0, None, ALU.is_lt))
                    step(v.tensor_tensor(p_, p_, c_, ALU.subtract))
                    step(v.scalar_tensor_tensor(blk[d][:, a:b], c_, float(NB), r_, ALU.mult, ALU.add))
            for k in (DST, SRC):
                if k == SRC:
                    dve.wait_ge(s_turn, EC // TC)
                step(v.tensor_copy(blk_f, blk[k][:, :]))
                v.engine_nop().then_inc(s_blkf, 1)
            step(v.scalar_tensor_tensor(field["cell"], blk[DST][:, :], float(NB), blk[SRC][:, :], ALU.mult, ALU.add))

            def equal(out_, ids, n, width):
                return v.tensor_tensor(out_, lane[0:out_.shape[0], 0:width].unsqueeze(1).to_broadcast([out_.shape[0], n, width]),
                                       ids.unsqueeze(2).to_broadcast([out_.shape[0], n, width]), ALU.is_equal)

            def count_onehots(i):
                for s in range(2):
                    wait_past(dve, s_cmm, i * 2 + (s - 1))
                    cols = ds(i * (2 * CC) + s * CC, CC)
                    equal(oh_count[s][0], blk[DST][:, cols], CC, NB)
                    equal(oh_count[s][1], blk[SRC][:, cols], CC, NB).then_inc(s_coh, 1)

            rounds(dve, COUNTS, count_onehots)
            dve.wait_ge(s_cnt, 1)
            step(v.tensor_copy(count[:, :], bank[0][0:NB, 0:NB]))
            tabs = [0]

            def product():
                tabs[0] += 1
                v.engine_nop().then_inc(s_tab, 1)
                dve.wait_ge(s_tabmm, tabs[0])

            kbits, tbits = K.bit_length() - 1, T.bit_length() - 1
            for o in (DST, SRC):
                if o == SRC:
                    product()
                    step(v.tensor_copy(count[:, :], bank[1][0:NB, 0:NB]))
                step(v.tensor_scalar(units_i[:, :], count[:, :], float(K - 1), None, ALU.add))
                step(v.tensor_scalar(units_i[:, :], units_i[:, :], kbits, None, ALU.arith_shift_right))
                step(v.tensor_copy(units[:, :], units_i[:, :]))
                step(v.tensor_tensor_scan(run[:, :], units[:, :], units[:, :], 0.0, ALU.add, ALU.max))
                step(v.tensor_scalar(tot_i[:, :], run[:, NB - 1:NB], float(T - 1), None, ALU.add))
                step(v.tensor_scalar(tot_i[:, :], tot_i[:, :], tbits, None, ALU.arith_shift_right))
                step(v.tensor_copy(tot[:, :], tot_i[:, :]))
                product()
                step(v.tensor_copy(start[:, :], bank[1][0:NB, 128:129]))
                step(v.tensor_tensor(run[:, :], run[:, :], units[:, :], ALU.subtract))
                step(v.tensor_scalar(tot[:, :], start[:, :], float(T), None, ALU.mult))
                step(v.tensor_scalar(first[o][:, :], run[:, :], tot[:, 0:1], None, ALU.add))
                step(v.tensor_scalar(begun[:, :], batch_no[:, :], start[:, 0:1], None, ALU.is_ge))
                product()
                step(v.tensor_scalar(batch_block[o][:, :], bank[7][0:1, 0:BATCHES], -1.0, None, ALU.add))
            product()
            step(v.tensor_tensor(run[:, :], bank[1][0:NB, 0:NB], first[DST][:, :], ALU.subtract))
            step(v.tensor_scalar(place[:, :], first[DST][:, :], float(K), None, ALU.mult))
            v.engine_nop().then_inc(s_shift, 1)
            dve.wait_ge(s_blkdram, 32)

            def rank_onehots(i, g):
                n = i * RS + g
                dve.wait_ge(s_load[g], i * 48 + 48)
                wait_past(dve, s_eq, (n - (RS - 1)) * RC)
                for k in range(2):
                    v.tensor_scalar(ohT[k][g], blk_row[k][g], here[0:NB, 0:1], None, ALU.is_equal)
                    m = equal(oh[k][g], blk[k][:, ds(n * RC, RC)], RC, NB)
                m.then_inc(s_roh, 1)

            def rank_finish(i, g, mark):
                n = i * RS + g
                dve.wait_ge(s_look, n + 1)
                v.tensor_tensor(place[:, :], place[:, :], bank[0][0:NB, 0:NB], ALU.add)
                mark(v.tensor_tensor(picked, bank[1][0:P, 0:RC * NB].rearrange("p (a b) -> p a b", b=NB), oh[SRC][g], ALU.mult))
                v.sem_inc(s_fin, 1)
                mark(v.tensor_reduce(seen[g], picked, AX.X, ALU.add))

            def rank_slots(i, g):
                n = i * RS + g
                dve.wait_ge(s_rank, n * RC + RC)
                wait_past(dve, s_scat[g], i * (16 * RC))
                v.tensor_tensor(at_stage[g], seen[g], rank[g], ALU.add).then_inc(s_at, 1)

            def rank_edges(i, mark):
                for g in range(RS):
                    rank_onehots(i, g)
                    if g > 0:
                        rank_finish(i, g - 1, mark)
                    elif not isinstance(i, int):
                        rank_finish(i - 1, RS - 1, mark)
                    if g > 1:
                        rank_slots(i, g - 2)
                    elif not isinstance(i, int):
                        rank_slots(i - 1, RS - 2 + g)

            stepped_rounds(TURNS, 2 * RS, rank_edges)
            rank_finish(TURNS - 1, RS - 1, step)
            rank_slots(TURNS - 1, RS - 2)
            rank_slots(TURNS - 1, RS - 1)
            dve.wait_ge(s_rank, TURNS * RS * RC)

            def degree_onehots(i):
                for s in range(2):
                    wait_past(dve, s_dmm, i * 2 + (s - 1))
                    cols = ds(i * (2 * CC) + s * CC, CC)
                    equal(deg_p[s], part[SRC][:, cols], CC, P)
                    equal(deg_b[s], blk[SRC][:, cols], CC, NB).then_inc(s_doh, 1)

            rounds(dve, COUNTS, degree_onehots)
            dve.wait_ge(s_deg, 1)
            step(v.tensor_copy(dinv[:, :], bank[4][0:P, 0:NB]))
            step(v.memset(AGG[:, :], 0.0))

            dve.wait_ge(s_gotu, GROUPS)
            dve.wait_ge(s_rowsu, GROUPS)
            step(v.tensor_scalar(valid, u_cell[:, :], float(CELLS), None, ALU.is_lt))
            step(v.tensor_scalar(target, u_shift[:, :], float(-U), None, ALU.add))
            step(v.tensor_tensor(target, target, valid, ALU.mult))
            step(v.scalar_tensor_tensor(target_i, target, float(U), u_here[:, :], ALU.add, ALU.add))
            step(v.tensor_tensor(u_shift[:, :], u_shift[:, :], u_here[:, :], ALU.add))
            step(v.tensor_tensor(source[DST][:, :], u_shift[:, :], valid, ALU.mult))
            step(v.tensor_copy(unit_meta[:, :, K:K + 1], u_here[:, :].unsqueeze(2)))
            step(v.tensor_copy(part_out.rearrange("p (t k) -> p t k", k=K), slot_part[DST][:, :, :]))
            v.sem_inc(s_target, 1)
            v.sem_inc(s_pout, 1)
            dve.wait_ge(s_mback, 16)
            dve.wait_ge(s_pdram, 16)
            step(v.tensor_copy(slot_part[SRC][:, :, :], unit_meta[:, :, 0:K]))
            step(v.tensor_copy(source[SRC][:, :].unsqueeze(2), unit_meta[:, :, K:K + 1]))
            step(v.tensor_copy(part_out.rearrange("p (t k) -> p t k", k=K), slot_part[SRC][:, :, :]))
            v.sem_inc(s_pout, 1)
            dve.wait_ge(s_pdram, 32)
            dve.wait_ge(s_x, 16)

            def blocks(a):
                return a.rearrange("p (b f) -> p b f", f=D)

            def per_node(a):
                return a.unsqueeze(2).to_broadcast([P, NB, D])

            X3, A3, H3, T3 = blocks(X[:, :]), blocks(AGG[:, :]), blocks(H), blocks(TMP[0:P, :])
            V3b = V3[:, :].rearrange("p (b f) -> p b f", f=W3)

            def cut_values(a):
                high, middle, low = (V3b[:, :, k * D:(k + 1) * D] for k in range(3))
                step(v.tensor_copy(high, a))
                step(v.tensor_tensor(T3, a, high, ALU.subtract))
                step(v.tensor_copy(middle, T3))
                step(v.tensor_tensor(low, T3, middle, ALU.subtract))
                v.sem_inc(s_value, 1)

            dve.wait_ge(s_filled, 48)
            cut_values(X3)
            sqrts = [0]

            def inverse_root(root):
                sqrts[0] += 1
                v.sem_inc(s_var, 1)
                dve.wait_ge(s_std, sqrts[0])
                step(v.reciprocal(root, root))

            def layernorm():
                step(v.tensor_reduce(stat[:, 0, :], X3, AX.X, ALU.add))
                step(v.tensor_scalar(stat[:, 0, :], stat[:, 0, :], 1.0 / D, None, ALU.mult))
                step(v.tensor_tensor(X3, X3, per_node(stat[:, 0, :]), ALU.subtract))
                step(v.tensor_tensor(T3, X3, X3, ALU.mult))
                step(v.tensor_reduce(stat[:, 1, :], T3, AX.X, ALU.add))
                step(v.tensor_scalar(stat[:, 1, :], stat[:, 1, :], 1.0 / D, EPS, ALU.mult, ALU.add))
                inverse_root(stat[:, 2, :])
                step(v.tensor_tensor(X3, X3, per_node(stat[:, 2, :]), ALU.mult))

            def transform(t, relu, out_):
                v.sem_inc(s_node, 1)

                def one_round(i):
                    o = out_[:, ds(i * (QB * D), QB * D)]
                    dve.wait_ge(s_mm, i + (t * QUADS + 1))
                    v.tensor_tensor(blocks(o), blocks(bank[4][0:P, 0:QB * D]),
                                    bias[:, t, :].unsqueeze(1).to_broadcast([P, QB, D]), ALU.add).then_inc(s_mmu, 1)

                rounds(dve, QUADS, one_round)
                dve.wait_ge(s_mmu, (t + 1) * QUADS)
                if relu:
                    step(v.tensor_scalar(out_, out_, 0.0, None, ALU.max))

            for q, (d, kind) in enumerate(PASSES):
                def selectors(i):
                    for s in range(2):
                        dve.wait_ge(s_prow[s], (i + (q * PAIRS + 1)) * 16)
                        for j in range(GB):
                            n = i * (2 * GB) + (s * GB + j + q * BATCHES)
                            wait_past(dve, s_spread, n - 1)
                            v.tensor_scalar(SEL[j % 2][0:P, :], part_row[s][:, j, :], here[0:P, 0:1], None,
                                            ALU.is_equal).then_inc(s_sel, 1)
                            if kind == "plain" and (j > 0 or s > 0 or not isinstance(i, int)):
                                copy_middle(i, s, j - 1)

                def copy_middle(i, s, j):
                    n = i * (2 * GB) + (s * GB + j)
                    dve.wait_ge(s_spread, n + (q * BATCHES + 1))
                    if j % GB == 0:
                        if not isinstance(i, int):
                            dve.wait_ge(s_store[s], i * 16 + 16 * PAIRS * q)
                    buf = s if j >= 0 else 1 - s
                    v.tensor_copy(msg3[buf][:, j % GB, 3 * W3:6 * W3], spread_bank(j % GB, 3)[:, 0:3 * W3]).then_inc(s_stage3, 1)

                rounds(dve, PAIRS, selectors)
                if kind == "plain":
                    copy_middle(PAIRS - 1, 1, GB - 1)
                dve.wait_ge(s_spread, (q + 1) * BATCHES)

                def reduce_pair(i, s, j):
                    m = i * GB + ((s * GB + j) // 2 + q * (BATCHES // 2))
                    dve.wait_ge(s_sum, i * (2 * GB) + (s * GB + j + 2 + q * BATCHES))
                    wait_past(dve, s_added, i * (2 * GB) + (s * GB + j - 2 + q * BATCHES))
                    v.tensor_reduce(pair_sum[j // 2 % 2], bank[6 + j // 2 % 2][0:P, 0:2 * W3]
                                    .rearrange("p (a c f) -> p a f c", a=2, c=3), AX.X, ALU.add).then_inc(s_reduced, 1)

                def add_sums(i, s, j, b):
                    n = i * (2 * GB) + (s * GB + j + q * BATCHES)
                    dve.wait_ge(s_reduced, i * GB + ((s * GB + j) // 2 + q * (BATCHES // 2) + 1))
                    wait_past(dve, s_added, n)
                    o = AGG[:, ds(b * D, D)]
                    v.tensor_tensor(o, o, pair_sum[j // 2 % 2][:, j % 2, :], ALU.add).then_inc(s_added, 1)

                def take_middle(s, j, t):
                    m3 = msg[s][:, j, :].rearrange("p (k f) -> p k f", f=D)
                    dve.wait_ge(s_high, t + (cut_before(q) + 1))
                    v.tensor_tensor(m3, m3, cut[j % 2][:, :, 0:D], ALU.subtract).then_inc(s_rest, 1)

                def collect(i, mark):
                    late = GB if isinstance(i, int) else 0
                    its_block = [None] * late + load_blocks(
                        dve, batch_regs[late:], batch_block[d][0:1, ds(i * (2 * GB) + (late - GB), 2 * GB - late)])
                    for s in range(2):
                        if kind != "plain":
                            dve.wait_ge(s_gath[s], (i + (q * PAIRS + 1)) * (16 * GB))
                        m4 = msg[s].rearrange("p t (k f) -> p t k f", f=D)
                        if kind == "edge":
                            dve.wait_ge(s_rows[s], (i + (PAIRS + 1)) * 16)
                            for j in range(GB):
                                m = v.tensor_tensor(m4[:, j], m4[:, j], rows[s][:, j, :, 0:D], ALU.add)
                            mark(m)
                            v.sem_inc(s_rowsu, 1)
                            v.sem_inc(s_msg, 1)
                        if kind == "weight":
                            for j in range(GB):
                                m = v.tensor_tensor(m4[:, j], m4[:, j],
                                                    w_s[:, ds(i * (2 * GB) + (s * GB + j), 1), :]
                                                    .rearrange("p a k -> p (a k)").unsqueeze(2).to_broadcast([128, K, D]), ALU.mult)
                            mark(m)
                            v.sem_inc(s_msg, 1)
                        for j in range(GB):
                            t = i * (2 * GB) + (s * GB + j)
                            before_i, before_s = (i, 0) if s else (i - 1, 1)
                            is_any = s > 0 or not isinstance(i, int)
                            if kind != "plain":
                                take_middle(s, j, t)
                            if j % 2 == 0 and is_any:
                                reduce_pair(before_i, before_s, j)
                            wait_past(dve, s_sum, t + (q * BATCHES - 1))
                            equal(onehot[j % 2], slot_part[d][:, ds(t, 1), :].rearrange("p a k -> p (a k)"), K, P)\
                                .then_inc(s_oh, 1)
                            if is_any:
                                add_sums(before_i, before_s, j, its_block[s * GB + j])
                stepped_rounds(PAIRS, 0 if kind == "plain" else 2, collect)
                last = load_blocks(dve, batch_regs[0:GB], batch_block[d][0:1, BATCHES - GB:BATCHES])
                for j in range(GB):
                    if j % 2 == 0:
                        reduce_pair(PAIRS - 1, 1, j)
                    add_sums(PAIRS - 1, 1, j, last[j])
                dve.wait_ge(s_added, (q + 1) * BATCHES)

                if q == 0:
                    dve.wait_ge(s_small, 16 * 9)
                    step(v.tensor_scalar(eps_sb[:, :], eps_sb[:, :], 1.0, None, ALU.add))
                    step(v.scalar_tensor_tensor(AGG[:, :], X[:, :], eps_sb[:, 0:1], AGG[:, :], ALU.mult, ALU.add))
                    step(v.tensor_tensor(X[:, :], X[:, :], AGG[:, :], ALU.add))
                    layernorm()
                    inverse_root(dinv[:, :])
                    step(v.tensor_tensor(H3, X3, per_node(dinv[:, :]), ALU.mult))
                elif q in (1, 2):
                    step(v.tensor_tensor(H, H, AGG[:, :], ALU.add))
                    step(v.tensor_tensor(H3, H3, per_node(dinv[:, :]), ALU.mult))
                    if q == 1:
                        step(v.tensor_tensor(H3, H3, per_node(dinv[:, :]), ALU.mult))
                    else:
                        step(v.tensor_tensor(X[:, :], X[:, :], H, ALU.add))
                        layernorm()
                elif q == 3:
                    transform(0, True, H)
                else:
                    transform(q - 3, q == 5, TMP[0:P, :])
                    step(v.tensor_tensor(X[:, :], X[:, :], TMP[0:P, :], ALU.add))
                    layernorm()
                if q < len(PASSES) - 1:
                    step(v.memset(AGG[:, :], 0.0))
                    cut_values(H3 if q in (0, 1, 3) else X3)
                else:
                    v.sem_inc(s_res, 1)


_INS = ["x", "src", "dst", "edge_attr_48", "edge_weight", "L0_gnn_eps", "L2_gnn_w_rel1", "L2_gnn_w_root1",
        "L2_gnn_b1", "L2_gnn_w_rel2", "L2_gnn_w_root2", "L2_gnn_b2", "L3_gnn_w", "L3_gnn_b"]


def kernel(**inputs):
    import numpy as _np
    import concourse.bacc as _bacc
    from concourse import mybir as _mybir
    from concourse.bass_utils import run_bass_kernel_spmd as _run

    nc = _bacc.Bacc("TRN2", target_bir_lowering=False, num_devices=1)
    arrays, args = {}, []
    for name in _INS:
        a = _np.ascontiguousarray(inputs[name])
        arrays[f"in_{name}_dram"] = a
        args.append(nc.dram_tensor(f"in_{name}_dram", a.shape, _mybir.dt.from_np(a.dtype), kind="ExternalInput").ap())
    args.append(nc.dram_tensor("out_0_dram", (N, D), F32, kind="ExternalOutput").ap())
    gnn_program(nc, *args)
    r = _run(nc, [arrays], core_ids=[0])
    return r.results[0]["out_0_dram"]
```
